# Optimizing a Trainium2 kernel written in Bass

```python
import numpy as np
import jax
import jax.numpy as jnp

def _softmax(x, axis=-1):
    return jax.nn.softmax(x, axis=axis)

def _gelu(x):
    return jax.nn.gelu(x, approximate=True)

def _silu(x):
    return jax.nn.silu(x)

def _sigmoid(x):
    return jax.nn.sigmoid(x)

def _layernorm(x, axis=-1, eps=1e-05):
    m = jnp.mean(x, axis=axis, keepdims=True)
    v = jnp.var(x, axis=axis, keepdims=True)
    return (x - m) / jnp.sqrt(v + eps)

def _scatter_add(tgt, idx, src, axis=0):
    return tgt.at[idx].add(src)

def _segment_sum(src, seg, n):
    return jax.ops.segment_sum(src, seg, n)
kernel_name = 'mk_flamingo_gated_d1_seqx_r8_0825c8'

def setup_inputs(seed: int=0):
    np.random.seed(seed)
    _w = jnp.asarray

    def _rec_inputs():
        import jax
        import jax.numpy as jnp
        _rk = jax.random.key(seed)
        x = -0.0003929 + 0.9999 * jax.random.normal(jax.random.fold_in(_rk, 1), (16, 64, 256), jnp.float32)
        _lenS = 64 - jax.random.randint(jax.random.fold_in(_rk, 7), (16,), 0, max(1, 64 // 4) + 1, jnp.int32)
        _lenS2 = 64 - jax.random.randint(jax.random.fold_in(_rk, 8), (16,), 0, max(1, 64 // 4) + 1, jnp.int32)
        _ctx_1024P = jax.random.normal(jax.random.fold_in(_rk, 11), (16, 16, 128), jnp.float32)
        _ctx_1024c = jax.random.dirichlet(jax.random.fold_in(_rk, 511), 0.3 * jnp.ones((16,), jnp.float32), (16, 64))
        _ctx_1024t = jnp.einsum('bsk,bkd->bsd', _ctx_1024c, _ctx_1024P)
        _ctx_1024t = _ctx_1024t * jax.lax.rsqrt(jnp.mean(jnp.square(_ctx_1024t)) + 1e-12) * 0.953939
        ctx_1024 = 0.000227908 + 0.99994 * (_ctx_1024t + 0.3 * jax.random.normal(jax.random.fold_in(_rk, 611), (16, 64, 128), jnp.float32))
        _g = jax.random.normal(jax.random.fold_in(_rk, 9001), (2, 1), jnp.float32)
        _g = jnp.sign(_g) * jnp.maximum(jnp.abs(_g), 1.0) + (_g == 0) * 1.0
        g_xattn = _g[0]
        g_ffn = _g[1]
        return (x, ctx_1024, g_xattn, g_ffn)
    x, ctx_1024, g_xattn, g_ffn = _rec_inputs()

    def _L0_xattn_setup():
        import jax, jax.numpy as jnp
        import numpy as np
        EPS = 1e-05

        def rmsnorm(x, g, eps=EPS):
            var = jnp.mean(jnp.square(x), axis=-1, keepdims=True)
            return x * jax.lax.rsqrt(var + eps) * g
        key = jax.random.key(seed)
        ks = jax.random.split(key, 8)
        B, Sq, Skv = (2, 512, 64)
        dim, cdim, H, D = (256, 128, 16, 128)
        inner = H * D
        s = lambda f: 1.0 / np.sqrt(f)
        return {'hidden_states': jax.random.normal(ks[0], (B, Sq, dim), jnp.float32), 'encoder_hidden_states': jax.random.normal(ks[1], (B, Skv, cdim), jnp.float32), 'Wq': jax.random.normal(ks[2], (dim, inner), jnp.float32) * s(dim), 'Wk': jax.random.normal(ks[3], (cdim, inner), jnp.float32) * s(cdim), 'Wv': jax.random.normal(ks[4], (cdim, inner), jnp.float32) * s(cdim), 'Wo': jax.random.normal(ks[5], (inner, dim), jnp.float32) * s(inner), 'gq': jnp.ones((D,), jnp.float32), 'gk': jnp.ones((D,), jnp.float32)}
    _L0_xattn_all = _L0_xattn_setup()
    _L0_xattn_in = {k: v for k, v in _L0_xattn_all.items() if k in ('Wq', 'Wk', 'Wv', 'Wo', 'gq', 'gk')}
    del _L0_xattn_all

    def _L0_ffn_setup():
        import jax, jax.numpy as jnp
        import numpy as np
        B, S, D = (2, 256, 256)
        H, HD = (16, 128)
        E, K, I = (16, 6, 176)
        SI = 352
        EPS = 1e-06

        def rmsnorm(x, w):
            v = jnp.mean(jnp.square(x), axis=-1, keepdims=True)
            return x * jax.lax.rsqrt(v + EPS) * w
        key = jax.random.key(seed)
        ks = jax.random.split(key, 14)
        s = 0.02
        return {'hidden_states': jax.random.normal(ks[0], (B, S, D), jnp.float32), 'ln1_w': jnp.ones((D,), jnp.float32), 'ln2_w': jnp.ones((D,), jnp.float32), 'wq': jax.random.normal(ks[1], (D, H * HD), jnp.float32) * s, 'wk': jax.random.normal(ks[2], (D, H * HD), jnp.float32) * s, 'wv': jax.random.normal(ks[3], (D, H * HD), jnp.float32) * s, 'wo': jax.random.normal(ks[4], (H * HD, D), jnp.float32) * s, 'gate_w': jax.random.normal(ks[5], (E, D), jnp.float32) * s, 'eg_w': jax.random.normal(ks[6], (E, I, D), jnp.float32) * s, 'eu_w': jax.random.normal(ks[7], (E, I, D), jnp.float32) * s, 'ed_w': jax.random.normal(ks[8], (E, D, I), jnp.float32) * s, 'sg_w': jax.random.normal(ks[9], (SI, D), jnp.float32) * s, 'su_w': jax.random.normal(ks[10], (SI, D), jnp.float32) * s, 'sd_w': jax.random.normal(ks[11], (D, SI), jnp.float32) * s}
    _L0_ffn_all = _L0_ffn_setup()
    _L0_ffn_in = {k: v for k, v in _L0_ffn_all.items() if k in ('ln1_w', 'ln2_w', 'wq', 'wk', 'wv', 'wo', 'gate_w', 'eg_w', 'eu_w', 'ed_w', 'sg_w', 'su_w', 'sd_w')}
    del _L0_ffn_all
    return {'x': x, 'ctx_1024': ctx_1024, 'g_xattn': g_xattn, 'g_ffn': g_ffn, 'L0_xattn_Wq': _L0_xattn_in['Wq'], 'L0_xattn_Wk': _L0_xattn_in['Wk'], 'L0_xattn_Wv': _L0_xattn_in['Wv'], 'L0_xattn_Wo': _L0_xattn_in['Wo'], 'L0_xattn_gq': _L0_xattn_in['gq'], 'L0_xattn_gk': _L0_xattn_in['gk'], 'L0_ffn_ln1_w': _L0_ffn_in['ln1_w'], 'L0_ffn_ln2_w': _L0_ffn_in['ln2_w'], 'L0_ffn_wq': _L0_ffn_in['wq'], 'L0_ffn_wk': _L0_ffn_in['wk'], 'L0_ffn_wv': _L0_ffn_in['wv'], 'L0_ffn_wo': _L0_ffn_in['wo'], 'L0_ffn_gate_w': _L0_ffn_in['gate_w'], 'L0_ffn_eg_w': _L0_ffn_in['eg_w'], 'L0_ffn_eu_w': _L0_ffn_in['eu_w'], 'L0_ffn_ed_w': _L0_ffn_in['ed_w'], 'L0_ffn_sg_w': _L0_ffn_in['sg_w'], 'L0_ffn_su_w': _L0_ffn_in['su_w'], 'L0_ffn_sd_w': _L0_ffn_in['sd_w']}

def reference(x, ctx_1024, g_xattn, g_ffn, L0_xattn_Wq, L0_xattn_Wk, L0_xattn_Wv, L0_xattn_Wo, L0_xattn_gq, L0_xattn_gk, L0_ffn_ln1_w, L0_ffn_ln2_w, L0_ffn_wq, L0_ffn_wk, L0_ffn_wv, L0_ffn_wo, L0_ffn_gate_w, L0_ffn_eg_w, L0_ffn_eu_w, L0_ffn_ed_w, L0_ffn_sg_w, L0_ffn_su_w, L0_ffn_sd_w):
    import jax
    import jax.numpy as jnp

    def _L0_xattn_ref(hidden_states, encoder_hidden_states, Wq, Wk, Wv, Wo, gq, gk):
        import jax, jax.numpy as jnp
        import numpy as np
        EPS = 1e-05

        def rmsnorm(x, g, eps=EPS):
            var = jnp.mean(jnp.square(x), axis=-1, keepdims=True)
            return x * jax.lax.rsqrt(var + eps) * g
        B, Sq, _ = hidden_states.shape
        Skv = encoder_hidden_states.shape[1]
        D = gq.shape[0]
        H = Wq.shape[1] // D
        scale = 1.0 / np.sqrt(D)
        q = (hidden_states @ Wq).reshape(B, Sq, H, D)
        k = (encoder_hidden_states @ Wk).reshape(B, Skv, H, D)
        v = (encoder_hidden_states @ Wv).reshape(B, Skv, H, D)
        q = rmsnorm(q, gq)
        k = rmsnorm(k, gk)
        scores = jnp.einsum('bqhd,bkhd->bhqk', q, k) * scale
        attn = jax.nn.softmax(scores, axis=-1)
        out = jnp.einsum('bhqk,bkhd->bqhd', attn, v)
        out = out.reshape(B, Sq, H * D)
        return out @ Wo

    def _L0_ffn_ref(hidden_states, ln1_w, ln2_w, wq, wk, wv, wo, gate_w, eg_w, eu_w, ed_w, sg_w, su_w, sd_w):
        import jax, jax.numpy as jnp
        import numpy as np
        B, S, D = (2, 256, 256)
        H, HD = (16, 128)
        E, K, I = (16, 6, 176)
        SI = 352
        EPS = 1e-06

        def rmsnorm(x, w):
            v = jnp.mean(jnp.square(x), axis=-1, keepdims=True)
            return x * jax.lax.rsqrt(v + EPS) * w
        b, s, d = hidden_states.shape
        x = hidden_states
        h = rmsnorm(x, ln1_w)
        q = (h @ wq).reshape(b, s, H, HD)
        k = (h @ wk).reshape(b, s, H, HD)
        v = (h @ wv).reshape(b, s, H, HD)
        scores = jnp.einsum('bqhd,bkhd->bhqk', q, k) / np.sqrt(HD).astype(np.float32)
        causal = jnp.tril(jnp.ones((s, s), bool))
        scores = jnp.where(causal, scores, jnp.float32(-1000000000.0))
        attn = jax.nn.softmax(scores, axis=-1)
        ao = jnp.einsum('bhqk,bkhd->bqhd', attn, v).reshape(b, s, H * HD) @ wo
        x = x + ao
        h = rmsnorm(x, ln2_w)
        t = h.reshape(-1, d)
        T = t.shape[0]
        logits = t @ gate_w.T
        probs = jax.nn.softmax(logits, axis=-1)
        topv, topi = jax.lax.top_k(probs, K)
        topv = topv / jnp.sum(topv, axis=-1, keepdims=True)
        cw = jnp.zeros((T, E), t.dtype).at[jnp.arange(T)[:, None], topi].add(topv)
        g = jnp.einsum('td,eid->eti', t, eg_w)
        u = jnp.einsum('td,eid->eti', t, eu_w)
        hh = jax.nn.silu(g) * u
        routed = jnp.einsum('eti,edi,te->td', hh, ed_w, cw)
        shared = jax.nn.silu(t @ sg_w.T) * (t @ su_w.T) @ sd_w.T
        out = x + (routed + shared).reshape(b, s, d)
        return out
    x = x + jnp.tanh(g_xattn[0]) * _L0_xattn_ref(_layernorm(x, axis=-1), ctx_1024, L0_xattn_Wq, L0_xattn_Wk, L0_xattn_Wv, L0_xattn_Wo, L0_xattn_gq, L0_xattn_gk)
    x = x + jnp.tanh(g_ffn[0]) * _L0_ffn_ref(_layernorm(x, axis=-1), L0_ffn_ln1_w, L0_ffn_ln2_w, L0_ffn_wq, L0_ffn_wk, L0_ffn_wv, L0_ffn_wo, L0_ffn_gate_w, L0_ffn_eg_w, L0_ffn_eu_w, L0_ffn_ed_w, L0_ffn_sg_w, L0_ffn_su_w, L0_ffn_sd_w)
    return x

_drawn_inputs = setup_inputs


def setup_inputs(seed=0):
    import zlib

    import numpy as np

    out = dict(_drawn_inputs(seed))
    spreads = {'L0_xattn_gq': (1.0, 0.2),
     'L0_xattn_gk': (1.0, 0.57),
     'L0_ffn_ln1_w': (1.0, 0.2),
     'L0_ffn_ln2_w': (1.0, 0.2)}
    factors = {}
    for name, (base, spread) in spreads.items():
        noise = np.random.default_rng([zlib.crc32(name.encode()), seed]).standard_normal(out[name].shape)
        drawn = base * np.exp(spread * noise) if base else spread * noise
        out[name] = jnp.asarray(drawn.astype(out[name].dtype))
    for name, factor in factors.items():
        out[name] = (out[name] * factor).astype(out[name].dtype)
    return out
```

```python
from contextlib import ExitStack

import concourse.bass as bass
from concourse import mybir

F32 = mybir.dt.float32
F32R = mybir.dt.float32r
ALU = mybir.AluOpType
ACT = mybir.ActivationFunctionType
AX = mybir.AxisListType.X

P = 128
LN_EXP = "natural_log_exp_and_others"
SEQ = 64
HALVES = 2


class Counter:

    def __init__(self, sem):
        self.sem, self.n = sem, 0

    def mark(self, instruction):
        instruction.then_inc(self.sem, 1)
        self.n += 1

    def link(self, engine, instruction):
        self.mark(instruction)
        engine.wait_ge(self.sem, self.n)


class Unit:

    def __init__(self, plan, kind, half, offset, j=0):
        self.plan, self.kind, self.half, self.offset, self.j = plan, kind, half, offset, j
        self.count = plan.counts[kind]
        self.i = j * 2 + offset
        before = half * self.count + offset
        self.parity = before % 2
        self.pair = j + before // 2
        self.static = isinstance(j, int)
        self.first = self.static and self.i == 0
        self.last = self.static and self.i == self.count - 1
        self.very_first = self.first and half == 0
        self.stage_number = plan.stages.index((kind, half))
        self.needs_tokens, self.tokens_number = self.first, self.stage_number + 1

    def next(self):
        if not self.last:
            return Unit(self.plan, self.kind, self.half, self.offset + 1, self.j)
        if self.stage_number + 1 < len(self.plan.stages):
            return Unit(self.plan, *self.plan.stages[self.stage_number + 1], 0)
        return None

    def prev(self):
        if not self.first:
            return Unit(self.plan, self.kind, self.half, self.offset - 1, self.j)
        if self.stage_number:
            kind, half = self.plan.stages[self.stage_number - 1]
            return Unit(self.plan, kind, half, self.plan.counts[kind] - 1)
        return None

    def done(self, back=0):
        return self.j * 2 + (self.half * self.count + self.offset + 1 - back)

    def loads(self):
        return self.pair * 16 + 16


class Plan:

    def __init__(self, stages, counts, pieces):
        self.stages, self.counts, self.pieces = stages, counts, pieces

    def piece(self, u):
        return self.pieces.get((u.kind, u.half, u.i), (None, None)) if u.static else (None, None)

    def run(self, engine, kind, half, body):
        beside = [i for k, h, i in self.pieces if (k, h) == (kind, half)]
        looped = (min(beside + [self.counts[kind] - 2]) - 1) // 2
        body(Unit(self, kind, half, 0))
        with engine.Fori(0, looped) as j:
            body(Unit(self, kind, half, 1, j))
            body(Unit(self, kind, half, 2, j))
        for i in range(1 + 2 * looped, self.counts[kind]):
            body(Unit(self, kind, half, i))


def plan_of(heads, chunks):
    pieces = {}

    def beside(kind, half, start, names, step):
        for n, name in enumerate(names.split()):
            pieces[kind, half, start + n] = (name, step)

    beside("a", 0, heads - 4, "stats norm turn", ("x", 1))
    beside("a", 1, heads - 5, "stats norm squares turn", ("y", 0))
    beside("b", 0, heads - 5, "stats norm squares turn", ("y", 1))
    beside("b", 1, heads - 8, "squares turn logits ranks ties weights spread", ("t", 0))
    beside("m", 0, chunks - 9, "squares turn logits ranks ties weights spread", ("t", 1))
    stages = [(kind, half) for kind in "abm" for half in range(HALVES)]
    return Plan(stages, {"a": heads, "b": heads, "m": chunks}, pieces)


def flamingo_layer(nc, x, ctx_t, ctx, head_a, head_b, chunk_m, small, out):
    TOK, D = x.shape
    H = head_a.shape[0]
    C = ctx.shape[1]
    CH = chunk_m.shape[0]
    E = 16
    SETUP = 6
    TOP = 6
    HT = TOK // HALVES
    NT = HT // P
    KD = D // P
    SPB = P // SEQ
    NS = HT // SEQ
    SCALE = float(P) ** -0.5
    R = E + 2
    assert C == P and D == 2 * P and HT == 512
    AQ, AK, AV, AO = 0, D, 0, C
    A1, A2 = D + P, C + D
    B1, B2 = 3 * D, D
    MG, MU, MS = 0, D, 2 * D
    M1, M2 = 2 * D + P, D
    SM_GQ, SM_GK, SM_LN1, SM_LN2, SM_GX, SM_GF, SM_GATE = 0, 1, 2, 4, 6, 7, 8
    SM_ID = SM_GATE + KD * E
    SM_MASK = SM_ID + P
    SM_TIE = SM_MASK + SEQ
    SM_W = SM_TIE + E * E

    with ExitStack() as stack:
        def sb(name, shape, dt=F32):
            return stack.enter_context(nc.sbuf_tensor(name, shape, dt))

        def psum(name):
            return stack.enter_context(nc.psum_tensor(name, [P, 512], F32))

        def sem(name):
            return stack.enter_context(nc.semaphore(name))

        sm = sb("sm", [P, SM_W])
        ident = sm[:, SM_ID:SM_ID + P]
        xs = sb("xs", [P, HALVES, NT, D])
        ys = sb("ys", [P, HALVES, NT, D])
        ctx_sb = sb("ctx_sb", [P, HALVES * NT, C])
        ctxt = sb("ctxt", [P, TOK])
        ctxt_hi, ctxt_lo = sb("ctxt_hi", [P, TOK], F32R), sb("ctxt_lo", [P, TOK], F32R)
        xt = sb("xt", [P, KD, HT])
        xt_hi = [sb(f"xt_hi{h}", [P, KD, HT], F32R) for h in range(HALVES)]
        xt_lo = [sb(f"xt_lo{h}", [P, KD, HT], F32R) for h in range(HALVES)]
        hn = sb("hn", [P, NT, D])
        ones = sb("ones", [P, P])
        zeros = sb("zeros", [P, 512], F32R)
        eps5, eps6 = sb("eps5", [P, 1]), sb("eps6", [P, 1])
        tg = sb("tg", [P, 2])
        gqk = sb("gqk", [P, 1])
        raw_a1 = [sb(f"raw_a1_{p}", [P, A1]) for p in range(2)]
        raw_a2 = [sb(f"raw_a2_{p}", [P, A2]) for p in range(2)]
        raw_b1 = [sb(f"raw_b1_{p}", [P, B1]) for p in range(2)]
        raw_b2 = [sb(f"raw_b2_{p}", [P, B2]) for p in range(2)]
        raw_m1 = [sb(f"raw_m1_{p}", [P, M1]) for p in range(2)]
        raw_m2 = [sb(f"raw_m2_{p}", [P, M2]) for p in range(2)]
        wq_hi, wq_lo = sb("wq_hi", [P, D], F32R), sb("wq_lo", [P, D], F32R)
        wk_hi, wk_lo = sb("wk_hi", [P, D], F32R), sb("wk_lo", [P, D], F32R)
        wv_hi, wv_lo = sb("wv_hi", [P, D], F32R), sb("wv_lo", [P, D], F32R)
        wo_hi, wo_lo = sb("wo_hi", [P, D], F32R), sb("wo_lo", [P, D], F32R)
        sel_hi = sb("sel_hi", [P, P], F32R)
        sq_q, sq_k = sb("sq_q", [P, HT]), sb("sq_k", [P, HT])
        qt, kt, vt = sb("qt", [P, HT]), sb("kt", [P, HT]), sb("vt", [P, HT])
        vs = sb("vs", [P, NT, P])
        ln_k, ln_q = sb("ln_k", [P, NT, SEQ]), sb("ln_q", [P, NT])
        ln_qk, r_qk = sb("ln_qk", [P, NT, SEQ]), sb("r_qk", [P, NT, SEQ])
        sc = sb("sc", [P, NT, SEQ])
        sc_max = sb("sc_max", [P, NT])
        sc_sub = sb("sc_sub", [P, NT, SEQ])
        ex = sb("ex", [P, NT, SEQ])
        ex_sum, ex_inv = sb("ex_sum", [P, NT]), sb("ex_inv", [P, NT])
        attn = sb("attn", [P, NT, P])
        attn_t = sb("attn_t", [P, HT])
        pv_hi, pv_lo = sb("pv_hi", [P, HT], F32R), sb("pv_lo", [P, HT], F32R)
        gs, gu, hh = sb("gs", [P, HT]), sb("gu", [P, HT]), sb("hh", [P, HT])
        cwt_hi = [sb(f"cwt_hi{h}", [R, HT], F32R) for h in range(HALVES)]
        cwt_lo = [sb(f"cwt_lo{h}", [R, HT], F32R) for h in range(HALVES)]
        bn = sb("bn", [P, NT, 6])
        mv = sb("mv", [P, NT, 2])
        ms = sb("ms", [P, NT])
        st = sb("st", [P, 8, NT])
        junk = sb("junk", [P, D])
        rt = sb("rt", [P, 6, NT, E])
        rmax = sb("rmax", [P, 4, NT])
        pair1, pair2 = sb("pair1", [P, NT, E, E]), sb("pair2", [P, NT, E, E])
        cw = sb("cw", [P, NT, R])

        acc = [psum("acc0"), psum("acc1")]
        bank_q, bank_k, bank_v = psum("bank_q"), psum("bank_k"), psum("bank_v")
        bank_s, bank_t, bank_p = psum("bank_s"), psum("bank_t"), psum("bank_p")

        ld_small, ld_ctx = sem("ld_small"), sem("ld_ctx")
        ld_x = [sem(f"ld_x{h}") for h in range(HALVES)]
        ld_a1 = [sem(f"ld_a1_{p}") for p in range(2)]
        ld_a2 = [sem(f"ld_a2_{p}") for p in range(2)]
        ld_b1 = [sem(f"ld_b1_{p}") for p in range(2)]
        ld_b2 = [sem(f"ld_b2_{p}") for p in range(2)]
        ld_m1 = [sem(f"ld_m1_{p}") for p in range(2)]
        ld_m2 = [sem(f"ld_m2_{p}") for p in range(2)]
        st_out = sem("st_out")

        def stage_sems(tag, names):
            return {n: sem(f"{tag}_{n}") for n in names.split()}

        A = stage_sems("a", "wq_hi wq_lo wk_hi wk_lo q_done k_done sq_q sq_k qt kt scores scaled max sub "
                       "exp sum inv norm_lo norm_hi t_done attn_t m_done m_hi m_lo ssk_done first_ssq ln_q ln_k "
                       "ln_qk r_qk pv_done pv_hi pv_lo wo_done")
        B = stage_sems("b", "wq_hi wq_lo wk_hi wk_lo wv_hi wv_lo wo_hi wo_lo q_done k_done v_done qt kt vt "
                       "vtr_done vs scores scaled max sub exp sum inv norm_lo norm_hi t_done attn_t "
                       "pv_done pv_hi pv_lo wo_done")
        M = stage_sems("m", "wg_hi wg_lo wu_hi wu_lo wd_hi wd_lo sel g_done u_done c_done silu gu hh hh_hi "
                       "hh_lo down")

        dve, act = Counter(sem("dve_step")), Counter(sem("act_step"))
        pe_tr = sem("pe_tr")
        pe_gate = sem("pe_gate")
        pe_cwt = sem("pe_cwt")
        tok_ready = sem("tok_ready")
        cw_ready = sem("cw_ready")
        var_ready, rough = sem("var_ready"), sem("rough")
        y_ready = sem("y_ready")
        xt_ready, xt_hi_ready, xt_lo_ready = sem("xt_ready"), sem("xt_hi_ready"), sem("xt_lo_ready")
        logits_sub, logits_exp = sem("logits_sub"), sem("logits_exp")
        cwt_hi_ready, cwt_lo_ready = sem("cwt_hi_ready"), sem("cwt_lo_ready")
        acc_free = sem("acc_free")
        setup_pool, setup_dve, setup_act = sem("setup_pool"), sem("setup_dve"), sem("setup_act")
        ctxt_hi_ready, ctxt_lo_ready = sem("ctxt_hi_ready"), sem("ctxt_lo_ready")
        out_ready = sem("out_ready")

        def tiles(ap):
            return ap.rearrange("p (t n) -> p t n", t=NT)

        stages = {"a": A, "b": B, "m": M}
        plan = plan_of(H, CH)
        STAGES = plan.stages
        PREP = {(step, half): n for n, (step, half) in enumerate((s_, h_) for s_ in "xyt" for h_ in range(HALVES))}
        piece_at, run_units = plan.piece, plan.run

        def first_unit(kind, half):
            return Unit(plan, kind, half, 0)

        def turn_banks(u):
            return (bank_p, bank_s if u.kind == "m" else bank_v)

        block = stack.enter_context(nc.Block())

        @block.sync
        def _(sp):
            x_v = x.rearrange("(h t p) d -> h p t d", h=HALVES, p=P)
            out_v = out.rearrange("(h t p) d -> h p t d", h=HALVES, p=P)

            def load_a1(u):
                sp.dma_start(raw_a1[u.parity][:], head_a[bass.ds(u.i, 1), :, 0:A1].rearrange("h p n -> p (h n)")).then_inc(ld_a1[u.parity], 16)

            def load_a2(u):
                sp.dma_start(raw_a2[u.parity][:], head_a[bass.ds(u.i, 1), :, A1:A1 + A2].rearrange("h p n -> p (h n)")).then_inc(ld_a2[u.parity], 16)

            def load_b1(u):
                sp.dma_start(raw_b1[u.parity][:], head_b[bass.ds(u.i, 1), :, 0:B1].rearrange("h p n -> p (h n)")).then_inc(ld_b1[u.parity], 16)

            def load_b2(u):
                sp.dma_start(raw_b2[u.parity][:], head_b[bass.ds(u.i, 1), :, B1:B1 + B2].rearrange("h p n -> p (h n)")).then_inc(ld_b2[u.parity], 16)

            def load_m1(u):
                sp.dma_start(raw_m1[u.parity][:], chunk_m[bass.ds(u.i, 1), :, 0:M1].rearrange("h p n -> p (h n)")).then_inc(ld_m1[u.parity], 16)

            def load_m2(u):
                sp.dma_start(raw_m2[u.parity][:], chunk_m[bass.ds(u.i, 1), :, M1:M1 + M2].rearrange("h p n -> p (h n)")).then_inc(ld_m2[u.parity], 16)

            sp.dma_start(xs[:, 0], x_v[0]).then_inc(ld_x[0], 16)
            sp.dma_start(sm[:], small).then_inc(ld_small, 16)
            sp.dma_start(ctxt[:], ctx_t).then_inc(ld_ctx, 16)
            sp.dma_start(ctx_sb[:], ctx.rearrange("(t p) c -> p t c", p=P)).then_inc(ld_ctx, 16)
            for i in range(2):
                load_a1(Unit(plan, "a", 0, i))
                load_a2(Unit(plan, "a", 0, i))
            sp.dma_start(xs[:, 1], x_v[1]).then_inc(ld_x[1], 16)
            for i in range(2):
                load_b1(Unit(plan, "b", 0, i))
                load_b2(Unit(plan, "b", 0, i))
                load_m1(Unit(plan, "m", 0, i))
                load_m2(Unit(plan, "m", 0, i))

            def refill(kind, half, loads):
                def unit(u):
                    for load, users in loads:
                        for user in users:
                            sp.wait_ge(user, u.done(2))
                        load(u)
                count = plan.counts[kind]
                start = 0 if half else 2
                pairs = (count - start) // 2
                with sp.Fori(0, pairs) as j:
                    unit(Unit(plan, kind, half, start, j))
                    unit(Unit(plan, kind, half, start + 1, j))
                if (count - start) % 2:
                    unit(Unit(plan, kind, half, count - 1))

            for half in range(HALVES):
                refill("a", half, [(load_a1, (A["wq_lo"], A["wk_lo"])), (load_a2, (A["m_done"],))])
            for half in range(HALVES):
                refill("b", half, [(load_b1, (B["wq_lo"], B["wk_lo"], B["wv_lo"])), (load_b2, (B["wo_lo"],))])
            for half in range(HALVES):
                refill("m", half, [(load_m1, (M["wg_lo"], M["wu_lo"], M["sel"])), (load_m2, (M["wd_lo"],))])
            for half in range(HALVES):
                sp.wait_ge(out_ready, half + 1)
                sp.dma_start(out_v[half], xs[:, half]).then_inc(st_out, 16)
            sp.wait_ge(st_out, 16 * HALVES)

        @block.tensor
        def _(pe):
            def project(bank, w_hi, w_lo, m_hi, m_lo, chunks=KD):
                n = 0
                for k in range(chunks):
                    cols = slice(k * P, (k + 1) * P)
                    for w, m in ((w_hi, m_hi), (w_hi, m_lo), (w_lo, m_hi)):
                        last = nc.tensor.matmul(bank[:], w[:, cols], m(k), start=n == 0, stop=n == 3 * chunks - 1)
                        n += 1
                return last

            def tokens_hi(u):
                return lambda k: xt_hi[u.half][:, k, :]

            def tokens_lo(u):
                return lambda k: xt_lo[u.half][:, k, :]

            def clear_acc(u):
                if u.stage_number:
                    pe.wait_ge(acc_free, u.stage_number)
                for bank in acc:
                    last = nc.tensor.matmul(bank[:], zeros[:, 0:P], zeros[:], start=True, stop=True, skip_group_check=True)

            def output(u):
                if u.kind == "a":
                    pe.wait_ge(A["pv_lo"], u.done())
                    pe.wait_ge(A["m_lo"], u.done())
                    done = A["wo_done"]
                elif u.kind == "b":
                    pe.wait_ge(B["pv_lo"], u.done())
                    pe.wait_ge(B["wo_lo"], u.done())
                    done = B["wo_done"]
                else:
                    pe.wait_ge(M["hh_lo"], u.done())
                    pe.wait_ge(M["wd_lo"], u.done())
                    done = M["down"]
                for t in range(NT):
                    tok = slice(t * P, (t + 1) * P)
                    for w, m in ((pv_hi, wo_hi), (pv_hi, wo_lo), (pv_lo, wo_hi)):
                        last = nc.tensor.matmul(acc[t // 2][:, (t % 2) * D:(t % 2 + 1) * D], w[:, tok], m[:],
                                                start=False, stop=True, skip_group_check=True)
                last.then_inc(done, 1)

            def project_first(u):
                if u.needs_tokens:
                    pe.wait_ge(xt_lo_ready, u.tokens_number)
                if u.kind == "a":
                    pe.wait_ge(A["wq_lo"], u.done())
                    project(bank_q, wq_hi, wq_lo, tokens_hi(u), tokens_lo(u)).then_inc(A["q_done"], 1)
                elif u.kind == "b":
                    pe.wait_ge(B["wq_lo"], u.done())
                    project(bank_q, wq_hi, wq_lo, tokens_hi(u), tokens_lo(u)).then_inc(B["q_done"], 1)
                else:
                    if not u.very_first:
                        pe.wait_ge(M["silu"], u.done(1))
                    pe.wait_ge(M["wg_lo"], u.done())
                    project(bank_q, wq_hi, wq_lo, tokens_hi(u), tokens_lo(u)).then_inc(M["g_done"], 1)
                    if not u.very_first:
                        pe.wait_ge(M["gu"], u.done(1))
                    pe.wait_ge(M["wu_lo"], u.done())
                    project(bank_k, wk_hi, wk_lo, tokens_hi(u), tokens_lo(u)).then_inc(M["u_done"], 1)
                    if u.needs_tokens:
                        pe.wait_ge(cwt_lo_ready, u.half + 1)
                    if not u.very_first:
                        pe.wait_ge(M["hh"], u.done(1))
                    pe.wait_ge(M["sel"], u.done())
                    nc.tensor.matmul(bank_v[:], sel_hi[0:R, :], cwt_hi[u.half][:], start=True, stop=False)
                    nc.tensor.matmul(bank_v[:], sel_hi[0:R, :], cwt_lo[u.half][:], start=False, stop=True)\
                        .then_inc(M["c_done"], 1)

            def project_keys(u):
                if u.kind == "a":
                    pe.wait_ge(A["wk_lo"], u.done())
                    if u.needs_tokens:
                        pe.wait_ge(ctxt_lo_ready, 1)
                    toks = slice(u.half * HT, (u.half + 1) * HT)
                    project(bank_k, wk_hi, wk_lo, lambda k: ctxt_hi[:, toks], lambda k: ctxt_lo[:, toks], 1)\
                        .then_inc(A["k_done"], 1)
                elif u.kind == "b":
                    pe.wait_ge(B["wk_lo"], u.done())
                    project(bank_k, wk_hi, wk_lo, tokens_hi(u), tokens_lo(u)).then_inc(B["k_done"], 1)

            def project_values(u):
                pe.wait_ge(B["wv_lo"], u.done())
                project(bank_v, wv_hi, wv_lo, tokens_hi(u), tokens_lo(u)).then_inc(B["v_done"], 1)

            def turn_values(u):
                pe.wait_ge(B["vt"], u.done())
                for t in range(NT):
                    last = nc.tensor.transpose(bank_t[:, t * P:(t + 1) * P], vt[:, t * P:(t + 1) * P], ident)
                last.then_inc(B["vtr_done"], 1)

            def value_out(u):
                pe.wait_ge(ld_a2[u.parity], u.loads())
                return nc.tensor.matmul(bank_v[:, 0:D], raw_a2[u.parity][:, AV:AV + C], raw_a2[u.parity][:, AO:AO + D],
                                        start=True, stop=True)

            def norm_q(u):
                pe.wait_ge(A["sq_q"], u.done())
                for t in range(NT):
                    last = nc.tensor.matmul(bank_v[:, D + t:D + t + 1], sq_q[:, t * P:(t + 1) * P], ones[:, 0:1],
                                            start=True, stop=True)
                return last

            def norm_k(u):
                pe.wait_ge(A["sq_k"], u.done())
                for b in range(NS):
                    t, s = b // SPB, b % SPB
                    last = nc.tensor.matmul(bank_s[s * SEQ:(s + 1) * SEQ, (NT + t) * SEQ:(NT + t + 1) * SEQ],
                                            ones[:, 0:SEQ], sq_k[:, b * SEQ:(b + 1) * SEQ], start=True, stop=True)
                last.then_inc(A["ssk_done"], 1)

            def scores(u):
                stage = stages[u.kind]
                pe.wait_ge(stage["qt"], u.done())
                pe.wait_ge(stage["kt"], u.done())
                if u.kind == "a":
                    pe.wait_ge(A["ln_k"], u.done())
                for b in range(NS):
                    tok = slice(b * SEQ, (b + 1) * SEQ)
                    t, s = b // SPB, b % SPB
                    last = nc.tensor.matmul(bank_s[s * SEQ:(s + 1) * SEQ, t * SEQ:(t + 1) * SEQ], qt[:, tok], kt[:, tok],
                                            start=True, stop=True)
                last.then_inc(stage["scores"], 1)

            def turn_attn(u):
                stage = stages[u.kind]
                pe.wait_ge(stage["norm_hi"], u.done())
                if u.kind == "b":
                    pe.wait_ge(B["vs"], u.done())
                for t in range(NT):
                    last = nc.tensor.transpose(bank_t[:, t * P:(t + 1) * P], attn[:, t, :], ident)
                last.then_inc(stage["t_done"], 1)

            def attn_values(u):
                stage = stages[u.kind]
                pe.wait_ge(stage["attn_t"], u.done())
                for t in range(NT):
                    value = ctx_sb[:, u.half * NT + t, :] if u.kind == "a" else vs[:, t, :]
                    last = nc.tensor.matmul(bank_p[:, t * P:(t + 1) * P], value, attn_t[:, t * P:(t + 1) * P],
                                            start=True, stop=True)
                last.then_inc(stage["pv_done"], 1)

            def turn_tokens(step, banks):
                pe.wait_ge(tok_ready, PREP[step] + 1)
                for k, bank in enumerate(banks):
                    for t in range(NT):
                        last = nc.tensor.transpose(bank[:, t * P:(t + 1) * P], hn[:, t, k * P:(k + 1) * P], ident)
                last.then_inc(pe_tr, 1)

            def prepare(u):
                piece, step = piece_at(u)
                if piece == "turn":
                    turn_tokens(step, turn_banks(u))
                    return [(xt_ready, PREP[step] + 1)]
                if piece == "logits":
                    pe.wait_ge(xt_ready, PREP[step] + 1)
                    for t in range(NT):
                        for k in range(KD):
                            last = nc.tensor.matmul(bank_p[:, t * E:(t + 1) * E], xt[:, k, t * P:(t + 1) * P],
                                                    sm[:, SM_GATE + k * E:SM_GATE + (k + 1) * E],
                                                    start=k == 0, stop=k == KD - 1)
                    last.then_inc(pe_gate, 1)
                    return [(logits_sub, step[1] + 1)]
                if piece == "spread":
                    pe.wait_ge(cw_ready, step[1] + 1)
                    for t in range(NT):
                        last = nc.tensor.transpose(bank_p[0:R, t * P:(t + 1) * P], cw[:, t, :], ident)
                    last.then_inc(pe_cwt, 1)
                    return [(cwt_lo_ready, step[1] + 1)]
                return []

            def head(u):
                prev, nxt = u.prev(), u.next()
                scores(u)
                project_first(nxt)
                if prev:
                    output(prev)
                held = prepare(u)
                project_keys(nxt)
                turn_attn(u)
                for semaphore, value in held:
                    pe.wait_ge(semaphore, value)
                if u.kind == "a":
                    m = value_out(u)
                    if nxt.kind == "a":
                        m = norm_q(nxt)
                    m.then_inc(A["m_done"], 1)
                    if nxt.kind == "a":
                        norm_k(nxt)
                if nxt.kind == "b":
                    if u.kind == "a":
                        pe.wait_ge(A["m_lo"], u.done())
                    project_values(nxt)
                attn_values(u)
                if nxt.kind == "b":
                    turn_values(nxt)
                if u.first:
                    clear_acc(u)

            def chunk(u):
                prev, nxt = u.prev(), u.next()
                if u.very_first:
                    output(prev)
                if nxt:
                    project_first(nxt)
                prepare(u)
                if u.first:
                    clear_acc(u)
                output(u)

            pe.wait_ge(ld_small, 16)
            pe.wait_ge(setup_pool, SETUP)
            turn_tokens(("x", 0), (bank_q, bank_k))
            start = first_unit("a", 0)
            project_first(start)
            project_keys(start)
            norm_q(start).then_inc(A["first_ssq"], 1)
            norm_k(start)
            for kind, half in STAGES:
                run_units(pe, kind, half, chunk if kind == "m" else head)

        @block.scalar
        def _(act_e):
            def rough_root(step):
                act_e.wait_ge(var_ready, PREP[step] + 1)
                act.link(act_e, nc.scalar.activation(st[:, 1, :], st[:, 0, :], ACT.Ln))
                nc.scalar.activation(st[:, 1, :], st[:, 1, :], ACT.Exp, scale=-0.5).then_inc(rough, 1)

            def mean_squares(source):
                for t in range(NT):
                    act.link(act_e, nc.scalar.activation(junk[:], source[:, t, :], ACT.Square, scale=float(D) ** -0.5,
                                                         accum_out=ms[:, t:t + 1]))
                act.link(act_e, nc.scalar.activation(st[:, 1, :], ms[:], ACT.Ln, bias=eps6[:, 0:1]))
                nc.scalar.activation(st[:, 1, :], st[:, 1, :], ACT.Exp, scale=-0.5).then_inc(rough, 1)

            def take_tokens(step, banks):
                kind, half = step
                act_e.wait_ge(pe_tr, PREP[step] + 1)
                if PREP[step]:
                    act_e.wait_ge(xt_lo_ready, PREP[step])
                for k, bank in enumerate(banks):
                    if kind == "x":
                        last = nc.scalar.activation(xt[:, k, :], bank[:], ACT.Copy)
                    else:
                        col = (SM_LN1 if kind == "y" else SM_LN2) + k
                        last = nc.scalar.activation(xt[:, k, :], bank[:], ACT.Identity, scale=sm[:, col:col + 1])
                last.then_inc(xt_ready, 1)

            def prepare(u):
                piece, step = piece_at(u)
                if piece == "norm":
                    rough_root(step)
                if piece == "squares":
                    if u.kind == "m":
                        act_e.preload_act_table_set(LN_EXP)
                    if step[0] == "y":
                        act_e.wait_ge(y_ready, step[1] + 1)
                    else:
                        act_e.wait_ge(acc_free, STAGES.index(("b", step[1])) + 1)
                    mean_squares(ys[:, step[1]])
                if piece == "turn":
                    take_tokens(step, turn_banks(u))
                if piece == "ranks":
                    act_e.wait_ge(logits_sub, step[1] + 1)
                    nc.scalar.activation(rt[:, 1], rt[:, 0], ACT.Exp).then_inc(logits_exp, 1)
                if piece == "spread":
                    act_e.wait_ge(pe_cwt, step[1] + 1)
                    nc.scalar.activation(cwt_hi[step[1]][:], bank_p[0:R, :], ACT.Copy).then_inc(cwt_hi_ready, 1)

            def square_q(u):
                act_e.wait_ge(A["q_done"], u.done())
                nc.scalar.activation(sq_q[:], bank_q[:], ACT.Square, scale=SCALE).then_inc(A["sq_q"], 1)

            def take_k(u):
                if u.kind == "a":
                    act_e.wait_ge(A["k_done"], u.done())
                    nc.scalar.activation(sq_k[:], bank_k[:], ACT.Square, scale=SCALE).then_inc(A["sq_k"], 1)
                    nc.scalar.activation(kt[:], bank_k[:], ACT.Identity, scale=gqk[:, 0:1]).then_inc(A["kt"], 1)
                if u.kind == "b":
                    act_e.wait_ge(B["k_done"], u.done())
                    nc.scalar.activation(kt[:], bank_k[:], ACT.Copy).then_inc(B["kt"], 1)

            def take_v(u):
                act_e.wait_ge(B["v_done"], u.done())
                nc.scalar.activation(vt[:], bank_v[:], ACT.Copy).then_inc(B["vt"], 1)

            def log_q(u):
                nc.scalar.activation(ln_q[:], bank_v[:, D:D + NT], ACT.Ln, bias=eps5[:, 0:1]).then_inc(A["ln_q"], 1)

            def log_k(u):
                act_e.wait_ge(A["ssk_done"], u.done())
                nc.scalar.activation(ln_k[:], tiles(bank_s[:, NT * SEQ:2 * NT * SEQ]), ACT.Ln, bias=eps5[:, 0:1])\
                    .then_inc(A["ln_k"], 1)

            def roots(u):
                act_e.wait_ge(A["ln_qk"], u.done())
                nc.scalar.activation(r_qk[:], ln_qk[:], ACT.Exp, scale=-0.5).then_inc(A["r_qk"], 1)

            def gate(u):
                act_e.wait_ge(M["g_done"], u.done())
                if not u.very_first:
                    act_e.wait_ge(M["gu"], u.done(1))
                nc.scalar.activation(gs[:], bank_q[:], ACT.Silu).then_inc(M["silu"], 1)

            def split_hidden(u):
                act_e.wait_ge(M["hh"], u.done())
                if u.very_first:
                    act_e.wait_ge(B["wo_done"], u.prev().done())
                else:
                    act_e.wait_ge(M["down"], u.done(1))
                nc.scalar.activation(pv_hi[:], hh[:], ACT.Copy).then_inc(M["hh_hi"], 1)

            def head(u):
                stage, nxt = stages[u.kind], u.next()
                act_e.wait_ge(stage["sub"], u.done())
                nc.scalar.activation(ex[:], sc_sub[:], ACT.Exp).then_inc(stage["exp"], 1)
                if nxt.kind == "a":
                    square_q(nxt)
                if nxt.kind == "m":
                    gate(nxt)
                prepare(u)
                take_k(nxt)
                act_e.wait_ge(stage["t_done"], u.done())
                nc.scalar.activation(attn_t[:], bank_t[:], ACT.Copy).then_inc(stage["attn_t"], 1)
                if u.kind == "a":
                    act_e.wait_ge(A["m_done"], u.done())
                    if nxt.kind == "a":
                        log_q(nxt)
                    nc.scalar.activation(wo_hi[:], bank_v[:, 0:D], ACT.Copy).then_inc(A["m_hi"], 1)
                    if nxt.kind == "a":
                        log_k(nxt)
                if nxt.kind == "b":
                    take_v(nxt)
                act_e.wait_ge(stage["pv_done"], u.done())
                nc.scalar.activation(pv_hi[:], bank_p[:], ACT.Copy).then_inc(stage["pv_hi"], 1)
                if nxt.kind == "a":
                    roots(nxt)

            def chunk(u):
                nxt = u.next()
                if u.very_first:
                    split_hidden(u)
                if nxt:
                    gate(nxt)
                prepare(u)
                if nxt:
                    split_hidden(nxt)

            act_e.wait_ge(ld_small, 16)
            act_e.wait_ge(setup_dve, 1)
            act_e.wait_ge(setup_pool, SETUP)
            nc.scalar.activation(tg[:], sm[:, SM_GX:SM_GF + 1], ACT.Tanh).then_inc(setup_act, 1)
            act_e.preload_act_table_set(LN_EXP)
            rough_root(("x", 0))
            act_e.wait_ge(ld_ctx, 32)
            nc.scalar.activation(ctxt_hi[:], ctxt[:], ACT.Copy).then_inc(ctxt_hi_ready, 1)
            take_tokens(("x", 0), (bank_q, bank_k))
            start = first_unit("a", 0)
            square_q(start)
            take_k(start)
            act_e.wait_ge(A["first_ssq"], 1)
            log_q(start)
            log_k(start)
            roots(start)
            for kind, half in STAGES:
                run_units(act_e, kind, half, chunk if kind == "m" else head)

        @block.vector
        def _(v):
            def link(ins):
                dve.link(v, ins)

            roots_taken = Counter(rough)

            def await_root():
                roots_taken.n += 1
                v.wait_ge(rough, roots_taken.n)

            def refined_root():
                link(nc.vector.tensor_tensor(st[:, 3, :], st[:, 0, :], st[:, 1, :], ALU.mult))
                link(nc.vector.tensor_tensor(st[:, 4, :], st[:, 3, :], st[:, 1, :], ALU.mult))
                link(nc.vector.tensor_scalar(st[:, 5, :], st[:, 4, :], -0.5, 1.5, ALU.mult, ALU.add))
                link(nc.vector.tensor_tensor(st[:, 2, :], st[:, 1, :], st[:, 5, :], ALU.mult))

            def per_expert(ap):
                return ap.unsqueeze(2).to_broadcast([P, NT, E])

            mine = rt[:, 2].unsqueeze(3).to_broadcast([P, NT, E, E])
            others = rt[:, 2].unsqueeze(2).to_broadcast([P, NT, E, E])

            def prepare_piece(piece, step):
                if not piece:
                    return
                kind, half = step
                if piece == "stats":
                    if kind == "x":
                        v.wait_ge(ld_x[half], 16)
                    for t in range(NT):
                        link(nc.vector.bn_stats(bn[:, t, :], xs[:, half, t, :]))
                    for t in range(NT):
                        link(nc.vector.bn_aggr(mv[:, t, :], bn[:, t, :]))
                    nc.vector.tensor_scalar(st[:, 0, :], mv[:, :, 1], 1e-5, None, ALU.add).then_inc(var_ready, 1)
                if piece == "norm":
                    await_root()
                    refined_root()
                    target, signal = (hn[:], tok_ready) if kind == "x" else (ys[:, half], y_ready)
                    if kind == "x" and PREP[step]:
                        v.wait_ge(pe_tr, PREP[step])
                    for t in range(NT):
                        last = nc.vector.tensor_scalar(target[:, t, :], xs[:, half, t, :], mv[:, t, 0:1],
                                                       st[:, 2, t:t + 1], ALU.subtract, ALU.mult)
                    last.then_inc(signal, 1)
                if piece == "squares":
                    await_root()
                    link(nc.vector.tensor_scalar(st[:, 0, :], ms[:], 1e-6, None, ALU.add))
                    refined_root()
                    v.wait_ge(pe_tr, PREP[step])
                    for t in range(NT):
                        last = nc.vector.tensor_scalar(hn[:, t, :], ys[:, half, t, :], st[:, 2, t:t + 1], None, ALU.mult)
                    last.then_inc(tok_ready, 1)
                if piece == "turn":
                    v.wait_ge(xt_ready, PREP[step] + 1)
                    nc.vector.tensor_copy(xt_hi[half][:], xt[:]).then_inc(xt_hi_ready, 1)
                if piece == "logits":
                    v.wait_ge(pe_gate, half + 1)
                    logits = bank_p[:, 0:NT * E].rearrange("p (t e) -> p t e", e=E)
                    link(nc.vector.tensor_reduce(rmax[:, 0, :], logits, AX, ALU.max))
                    nc.vector.tensor_tensor(rt[:, 0], logits, per_expert(rmax[:, 0, :]), ALU.subtract).then_inc(logits_sub, 1)
                if piece == "ranks":
                    v.wait_ge(logits_exp, half + 1)
                    link(nc.vector.tensor_reduce(rmax[:, 1, :], rt[:, 1], AX, ALU.add))
                    link(nc.vector.reciprocal(rmax[:, 2, :], rmax[:, 1, :]))
                    link(nc.vector.tensor_tensor(rt[:, 2], rt[:, 1], per_expert(rmax[:, 2, :]), ALU.mult))
                    link(nc.vector.tensor_tensor(pair1[:], others, mine, ALU.is_equal))
                if piece == "ties":
                    tie = sm[:, SM_TIE:SM_TIE + E * E].rearrange("p (e f) -> p e f", f=E).unsqueeze(1)
                    link(nc.vector.tensor_tensor(pair1[:], pair1[:], tie.to_broadcast([P, NT, E, E]), ALU.mult))
                    link(nc.vector.tensor_tensor(pair2[:], others, mine, ALU.is_gt))
                if piece == "weights":
                    link(nc.vector.tensor_tensor(pair1[:], pair1[:], pair2[:], ALU.add))
                    link(nc.vector.tensor_reduce(rt[:, 3], pair1[:], AX, ALU.add))
                    link(nc.vector.tensor_scalar(rt[:, 4], rt[:, 3], float(TOP), None, ALU.is_lt))
                    link(nc.vector.tensor_tensor(rt[:, 5], rt[:, 4], rt[:, 2], ALU.mult))
                    link(nc.vector.tensor_reduce(rmax[:, 3, :], rt[:, 5], AX, ALU.add))
                    link(nc.vector.reciprocal(rmax[:, 1, :], rmax[:, 3, :]))
                    nc.vector.tensor_tensor(cw[:, :, 0:E], rt[:, 5], per_expert(rmax[:, 1, :]), ALU.mult).then_inc(cw_ready, 1)
                if piece == "spread":
                    v.wait_ge(cwt_hi_ready, half + 1)
                    nc.vector.tensor_tensor(cwt_lo[half][:], bank_p[0:R, :], cwt_hi[half][:], ALU.subtract)\
                        .then_inc(cwt_lo_ready, 1)

            def softmax(u):
                stage = stages[u.kind]
                if u.kind == "a":
                    v.wait_ge(A["r_qk"], u.done())
                v.wait_ge(stage["scores"], u.done())
                found = tiles(bank_s[:, 0:NT * SEQ])
                if u.kind == "a":
                    nc.vector.tensor_tensor(sc[:], found, r_qk[:], ALU.mult).then_inc(A["scaled"], 1)
                else:
                    mask = sm[:, SM_MASK:SM_MASK + SEQ].unsqueeze(1).to_broadcast([P, NT, SEQ])
                    nc.vector.scalar_tensor_tensor(sc[:], found, SCALE, mask, ALU.mult, ALU.add).then_inc(B["scaled"], 1)
                v.wait_ge(stage["scaled"], u.done())
                nc.vector.tensor_reduce(sc_max[:], sc[:], AX, ALU.max).then_inc(stage["max"], 1)
                v.wait_ge(stage["max"], u.done())
                nc.vector.tensor_tensor(sc_sub[:], sc[:], sc_max[:].unsqueeze(2).to_broadcast([P, NT, SEQ]),
                                        ALU.subtract).then_inc(stage["sub"], 1)
                v.wait_ge(stage["exp"], u.done())
                nc.vector.tensor_reduce(ex_sum[:], ex[:], AX, ALU.add).then_inc(stage["sum"], 1)
                v.wait_ge(stage["sum"], u.done())
                nc.vector.reciprocal(ex_inv[:], ex_sum[:]).then_inc(stage["inv"], 1)
                v.wait_ge(stage["inv"], u.done())
                for s, signal in ((0, stage["norm_lo"]), (1, stage["norm_hi"])):
                    rows = slice(s * SEQ, (s + 1) * SEQ)
                    nc.vector.tensor_tensor(attn[rows, :, s * SEQ:(s + 1) * SEQ], ex[rows],
                                            ex_inv[rows].unsqueeze(2).to_broadcast([SEQ, NT, SEQ]), ALU.mult)\
                        .then_inc(signal, 1)

            def take_q(u):
                if u.kind == "a":
                    v.wait_ge(A["sq_q"], u.done())
                    nc.vector.tensor_copy(qt[:], bank_q[:]).then_inc(A["qt"], 1)
                if u.kind == "b":
                    v.wait_ge(B["q_done"], u.done())
                    nc.vector.tensor_copy(qt[:], bank_q[:]).then_inc(B["qt"], 1)

            def split_first(u, user):
                if user:
                    v.wait_ge(M["g_done"] if user.kind == "m" else stages[user.kind]["q_done"], user.done())
                if u.kind == "a":
                    v.wait_ge(ld_a1[u.parity], u.loads())
                    nc.vector.tensor_copy(wq_hi[:], raw_a1[u.parity][:, AQ:AQ + D]).then_inc(A["wq_hi"], 1)
                elif u.kind == "b":
                    v.wait_ge(ld_b1[u.parity], u.loads())
                    nc.vector.tensor_copy(wq_hi[:], raw_b1[u.parity][:, 0:D]).then_inc(B["wq_hi"], 1)
                else:
                    v.wait_ge(ld_m1[u.parity], u.loads())
                    nc.vector.tensor_copy(wq_hi[:], raw_m1[u.parity][:, MG:MG + D]).then_inc(M["wg_hi"], 1)

            def split_second(u, user):
                if user:
                    v.wait_ge(M["u_done"] if user.kind == "m" else stages[user.kind]["k_done"], user.done())
                if u.kind == "a":
                    nc.vector.tensor_copy(wk_hi[:, 0:P], raw_a1[u.parity][:, AK:AK + P]).then_inc(A["wk_hi"], 1)
                elif u.kind == "b":
                    nc.vector.tensor_copy(wk_hi[:], raw_b1[u.parity][:, D:2 * D]).then_inc(B["wk_hi"], 1)
                else:
                    nc.vector.tensor_copy(wk_hi[:], raw_m1[u.parity][:, MU:MU + D]).then_inc(M["wu_hi"], 1)

            def split_select(u, user):
                if user.kind == "m":
                    v.wait_ge(M["c_done"], user.done())
                nc.vector.tensor_copy(sel_hi[0:R, :], raw_m1[u.parity][0:R, MS:MS + P]).then_inc(M["sel"], 1)

            def split_values(u, user):
                if user.kind == "b":
                    v.wait_ge(B["v_done"], user.done())
                nc.vector.tensor_copy(wv_hi[:], raw_b1[u.parity][:, 2 * D:3 * D]).then_inc(B["wv_hi"], 1)

            def split_out(u):
                prev = u.prev()
                if u.kind == "b":
                    v.wait_ge(stages[prev.kind]["wo_done"], prev.done())
                    v.wait_ge(ld_b2[u.parity], u.loads())
                    nc.vector.tensor_copy(wo_hi[:], raw_b2[u.parity][:]).then_inc(B["wo_hi"], 1)
                else:
                    v.wait_ge(M["down"] if prev.kind == "m" else B["wo_done"], prev.done())
                    v.wait_ge(ld_m2[u.parity], u.loads())
                    nc.vector.tensor_copy(wo_hi[:], raw_m2[u.parity][:]).then_inc(M["wd_hi"], 1)

            def gated(u):
                v.wait_ge(M["u_done"], u.done())
                v.wait_ge(M["silu"], u.done())
                nc.vector.tensor_tensor(gu[:], bank_k[:], gs[:], ALU.mult).then_inc(M["gu"], 1)

            def weighted(u):
                v.wait_ge(M["c_done"], u.done())
                v.wait_ge(M["gu"], u.done())
                if not u.very_first:
                    v.wait_ge(M["hh_hi"], u.done(1))
                nc.vector.tensor_tensor(hh[:], bank_v[:], gu[:], ALU.mult).then_inc(M["hh"], 1)

            def split_hidden(u):
                v.wait_ge(M["hh_hi"], u.done())
                nc.vector.tensor_tensor(pv_lo[:], hh[:], pv_hi[:], ALU.subtract).then_inc(M["hh_lo"], 1)

            def read_acc(last):
                kind, half = last.kind, last.half
                v.wait_ge(stages[kind]["down" if kind == "m" else "wo_done"], last.done())
                for b in range(2):
                    two = slice(2 * b, 2 * b + 2)
                    part = acc[b][:].rearrange("p (t d) -> p t d", d=D)
                    if kind == "a":
                        add = nc.vector.scalar_tensor_tensor(xs[:, half, two], part, tg[:, 0:1], xs[:, half, two],
                                                             ALU.mult, ALU.add)
                    else:
                        add = nc.vector.tensor_tensor(ys[:, half, two], part, ys[:, half, two], ALU.add)
                add.then_inc(acc_free, 1)
                v.wait_ge(acc_free, STAGES.index((kind, half)) + 1)

            def finish(half):
                nc.vector.scalar_tensor_tensor(xs[:, half], ys[:, half], tg[:, 1:2], xs[:, half],
                                               ALU.mult, ALU.add).then_inc(out_ready, 1)

            def head(u):
                prev, nxt = u.prev(), u.next()
                after = nxt.next()
                softmax(u)
                take_q(nxt)
                if nxt.kind == "m":
                    gated(nxt)
                split_first(after, nxt)
                split_second(after, nxt)
                if nxt.kind == "m":
                    weighted(nxt)
                    split_select(after, nxt)
                elif after.kind == "m":
                    split_select(after, nxt)
                if u.first and prev:
                    read_acc(prev)
                prepare_piece(*piece_at(u))
                if u.kind == "b":
                    split_out(u)
                if u.kind == "a":
                    v.wait_ge(A["m_hi"], u.done())
                    nc.vector.tensor_tensor(wo_lo[:], bank_v[:, 0:D], wo_hi[:], ALU.subtract).then_inc(A["m_lo"], 1)
                if after.kind == "b":
                    split_values(after, nxt)
                if nxt.kind == "b":
                    v.wait_ge(B["vtr_done"], nxt.done())
                    nc.vector.tensor_copy(vs[:], tiles(bank_t[:])).then_inc(B["vs"], 1)
                v.wait_ge(stages[u.kind]["pv_hi"], u.done())
                nc.vector.tensor_tensor(pv_lo[:], bank_p[:], pv_hi[:], ALU.subtract).then_inc(stages[u.kind]["pv_lo"], 1)

            def chunk(u):
                nxt = u.next()
                after = nxt.next() if nxt else None
                if u.very_first:
                    read_acc(u.prev())
                    split_hidden(u)
                    split_out(u)
                if nxt:
                    gated(nxt)
                if after:
                    split_first(after, nxt)
                    split_second(after, nxt)
                if nxt:
                    weighted(nxt)
                if after:
                    split_select(after, nxt)
                prepare_piece(*piece_at(u))
                if u.last:
                    read_acc(u)
                if nxt:
                    split_hidden(nxt)
                    split_out(nxt)
                if u.last:
                    finish(u.half)

            v.wait_ge(ld_small, 16)
            v.wait_ge(setup_pool, SETUP)
            nc.vector.scalar_tensor_tensor(gqk[:], sm[:, SM_GQ:SM_GQ + 1], SCALE, sm[:, SM_GK:SM_GK + 1],
                                           ALU.mult, ALU.mult).then_inc(setup_dve, 1)
            v.wait_ge(setup_act, 1)
            prepare_piece("stats", ("x", 0))
            prepare_piece("norm", ("x", 0))
            start = first_unit("a", 0)
            split_first(start, None)
            split_second(start, None)
            prepare_piece("turn", ("x", 0))
            take_q(start)
            split_first(start.next(), start)
            split_second(start.next(), start)
            for kind, half in STAGES:
                run_units(v, kind, half, chunk if kind == "m" else head)

        @block.gpsimd
        def _(pool):
            def rest(lo, raw, hi, signal):
                nc.gpsimd.tensor_tensor(lo, raw, hi, ALU.subtract).then_inc(signal, 1)

            def split_first(u):
                if u.kind == "a":
                    pool.wait_ge(A["wq_hi"], u.done())
                    rest(wq_lo[:], raw_a1[u.parity][:, AQ:AQ + D], wq_hi[:], A["wq_lo"])
                elif u.kind == "b":
                    pool.wait_ge(B["wq_hi"], u.done())
                    rest(wq_lo[:], raw_b1[u.parity][:, 0:D], wq_hi[:], B["wq_lo"])
                else:
                    pool.wait_ge(M["wg_hi"], u.done())
                    rest(wq_lo[:], raw_m1[u.parity][:, MG:MG + D], wq_hi[:], M["wg_lo"])

            def split_second(u):
                if u.kind == "a":
                    pool.wait_ge(A["wk_hi"], u.done())
                    rest(wk_lo[:, 0:P], raw_a1[u.parity][:, AK:AK + P], wk_hi[:, 0:P], A["wk_lo"])
                elif u.kind == "b":
                    pool.wait_ge(B["wk_hi"], u.done())
                    rest(wk_lo[:], raw_b1[u.parity][:, D:2 * D], wk_hi[:], B["wk_lo"])
                else:
                    pool.wait_ge(M["wu_hi"], u.done())
                    rest(wk_lo[:], raw_m1[u.parity][:, MU:MU + D], wk_hi[:], M["wu_lo"])

            def split_values(u):
                pool.wait_ge(B["wv_hi"], u.done())
                rest(wv_lo[:], raw_b1[u.parity][:, 2 * D:3 * D], wv_hi[:], B["wv_lo"])

            def split_out(u):
                if u.kind == "b":
                    pool.wait_ge(B["wo_hi"], u.done())
                    rest(wo_lo[:], raw_b2[u.parity][:], wo_hi[:], B["wo_lo"])
                else:
                    pool.wait_ge(M["wd_hi"], u.done())
                    rest(wo_lo[:], raw_m2[u.parity][:], wo_hi[:], M["wd_lo"])

            def split_tokens(step):
                pool.wait_ge(xt_hi_ready, PREP[step] + 1)
                for k in range(KD):
                    last = nc.gpsimd.tensor_tensor(xt_lo[step[1]][:, k, :], xt[:, k, :], xt_hi[step[1]][:, k, :], ALU.subtract)
                last.then_inc(xt_lo_ready, 1)

            def prepare(u):
                piece, step = piece_at(u)
                if piece == "turn":
                    split_tokens(step)

            def add_logs(u):
                pool.wait_ge(A["ln_k"], u.done())
                nc.gpsimd.tensor_tensor(ln_qk[:], ln_k[:], ln_q[:].unsqueeze(2).to_broadcast([P, NT, SEQ]), ALU.add)\
                    .then_inc(A["ln_qk"], 1)

            def head(u):
                nxt = u.next()
                after = nxt.next()
                split_first(after)
                split_second(after)
                if u.kind == "b":
                    split_out(u)
                if after.kind == "b":
                    split_values(after)
                if nxt.kind == "a":
                    add_logs(nxt)
                prepare(u)

            def chunk(u):
                nxt = u.next()
                after = nxt.next() if nxt else None
                if u.very_first:
                    split_out(u)
                if after:
                    split_first(after)
                    split_second(after)
                if nxt:
                    split_out(nxt)
                prepare(u)

            nc.gpsimd.memset(zeros[:].bitcast(F32), 0.0).then_inc(setup_pool, 1)
            nc.gpsimd.memset(ones[:], 1.0).then_inc(setup_pool, 1)
            nc.gpsimd.memset(attn[:], 0.0).then_inc(setup_pool, 1)
            nc.gpsimd.memset(eps5[:], 1e-5).then_inc(setup_pool, 1)
            nc.gpsimd.memset(eps6[:], 1e-6).then_inc(setup_pool, 1)
            nc.gpsimd.memset(cw[:, :, E:R], 1.0).then_inc(setup_pool, 1)
            pool.wait_ge(ctxt_hi_ready, 1)
            rest(ctxt_lo[:], ctxt[:], ctxt_hi[:], ctxt_lo_ready)
            start = first_unit("a", 0)
            split_first(start)
            split_second(start)
            split_tokens(("x", 0))
            split_first(start.next())
            split_second(start.next())
            add_logs(start)
            for kind, half in STAGES:
                run_units(pool, kind, half, chunk if kind == "m" else head)


_INS = ["x", "ctx_t", "ctx", "head_a", "head_b", "chunk_m", "small"]


def lay_out(i, np):
    a = {k: np.asarray(v) for k, v in i.items()}
    f = np.float32
    x = a["x"].reshape(-1, a["x"].shape[-1])
    D = x.shape[1]
    ctx = a["ctx_1024"].reshape(x.shape[0], -1)
    C = ctx.shape[1]
    K = D // P

    def in_heads(w, chunks):
        h = w.shape[1] // P
        return w.reshape(chunks, P, h, P).transpose(2, 1, 0, 3).reshape(h, P, chunks * P)

    def out_heads(w):
        return w.reshape(-1, P, w.shape[1])

    wv_t = a["L0_xattn_Wv"].reshape(C, -1, P).transpose(1, 2, 0)
    head_a = np.concatenate([in_heads(a["L0_xattn_Wq"], K), in_heads(a["L0_xattn_Wk"], 1), wv_t,
                             out_heads(a["L0_xattn_Wo"])], axis=2)
    head_b = np.concatenate([in_heads(a["L0_ffn_wq"], K), in_heads(a["L0_ffn_wk"], K), in_heads(a["L0_ffn_wv"], K),
                             out_heads(a["L0_ffn_wo"])], axis=2)
    E, I, _ = a["L0_ffn_eg_w"].shape
    hidden = E * I + a["L0_ffn_sg_w"].shape[0]
    chunks = -(-hidden // P)
    pad = np.zeros((chunks * P - hidden, D), f)
    gate = np.concatenate([a["L0_ffn_eg_w"].reshape(-1, D), a["L0_ffn_sg_w"], pad])
    up = np.concatenate([a["L0_ffn_eu_w"].reshape(-1, D), a["L0_ffn_su_w"], pad])
    down = np.concatenate([a["L0_ffn_ed_w"].transpose(0, 2, 1).reshape(-1, D), a["L0_ffn_sd_w"].T, pad])
    unit = np.arange(chunks * P)
    select = np.zeros((P, chunks * P), f)
    for e in range(hidden // I):
        select[e] = unit // I == e
    chunk_m = np.concatenate([in_heads(gate.T, K), in_heads(up.T, K), select.reshape(P, chunks, P).transpose(1, 0, 2),
                              down.reshape(chunks, P, D)], axis=2)
    query, key = np.arange(P)[:, None] % SEQ, np.arange(SEQ)[None]
    mask = np.where(key <= query, f(0), f(-1e30)).astype(f)
    tie = np.tril(np.ones((E, E), f), -1).reshape(1, -1)
    small = np.concatenate([
        a["L0_xattn_gq"].reshape(P, 1), a["L0_xattn_gk"].reshape(P, 1),
        a["L0_ffn_ln1_w"].reshape(K, P).T, a["L0_ffn_ln2_w"].reshape(K, P).T,
        np.broadcast_to(a["g_xattn"].reshape(1, 1), (P, 1)), np.broadcast_to(a["g_ffn"].reshape(1, 1), (P, 1)),
        a["L0_ffn_gate_w"].T.reshape(K, P, E).transpose(1, 0, 2).reshape(P, K * E),
        np.eye(P, dtype=f), mask, np.broadcast_to(tie, (P, E * E))], axis=1)
    return {"x": x, "ctx_t": ctx.T, "ctx": ctx, "head_a": head_a, "head_b": head_b, "chunk_m": chunk_m, "small": small}


def kernel(**inputs):
    import concourse.bacc as bacc
    import numpy as np
    from concourse.bass_utils import run_bass_kernel_spmd

    laid = {k: np.ascontiguousarray(v) for k, v in lay_out(inputs, np).items()}
    nc = bacc.Bacc("TRN2", target_bir_lowering=False, num_devices=1)
    aps = [nc.dram_tensor(f"in_{n}", laid[n].shape, mybir.dt.from_np(laid[n].dtype), kind="ExternalInput").ap() for n in _INS]
    out = nc.dram_tensor("out", laid["x"].shape, F32, kind="ExternalOutput").ap()
    flamingo_layer(nc, *aps, out)
    r = run_bass_kernel_spmd(nc, [{f"in_{n}": laid[n] for n in _INS}], core_ids=[0])
    return r.results[0]["out"].reshape(inputs["x"].shape)
```

```python
from contextlib import ExitStack

import concourse.bass as bass
from concourse import mybir

F32 = mybir.dt.float32
F32R = mybir.dt.float32r
ALU = mybir.AluOpType
ACT = mybir.ActivationFunctionType
AX = mybir.AxisListType.X

P = 128
LN_EXP = "natural_log_exp_and_others"
SEQ = 64
HALVES = 2


class Counter:

    def __init__(self, sem):
        self.sem, self.n = sem, 0

    def mark(self, instruction):
        instruction.then_inc(self.sem, 1)
        self.n += 1

    def link(self, engine, instruction):
        self.mark(instruction)
        engine.wait_ge(self.sem, self.n)


class Unit:

    def __init__(self, plan, kind, half, offset, j=0):
        self.plan, self.kind, self.half, self.offset, self.j = plan, kind, half, offset, j
        self.count = plan.counts[kind]
        self.i = j * 2 + offset
        before = half * self.count + offset
        self.parity = before % 2
        self.pair = j + before // 2
        self.static = isinstance(j, int)
        self.first = self.static and self.i == 0
        self.last = self.static and self.i == self.count - 1
        self.very_first = self.first and half == 0
        self.deferred = kind == "a" and not (self.last and half == HALVES - 1)
        self.in_first_pair = self.static and self.i < 2 and half == 0
        self.stage_number = plan.stages.index((kind, half))
        self.needs_tokens, self.tokens_number = self.first, self.stage_number + 1

    def next(self):
        if not self.last:
            return Unit(self.plan, self.kind, self.half, self.offset + 1, self.j)
        if self.stage_number + 1 < len(self.plan.stages):
            return Unit(self.plan, *self.plan.stages[self.stage_number + 1], 0)
        return None

    def prev(self):
        if not self.first:
            return Unit(self.plan, self.kind, self.half, self.offset - 1, self.j)
        if self.stage_number:
            kind, half = self.plan.stages[self.stage_number - 1]
            return Unit(self.plan, kind, half, self.plan.counts[kind] - 1)
        return None

    def done(self, back=0):
        return self.j * 2 + (self.half * self.count + self.offset + 1 - back)

    def loads(self):
        return self.pair * 16 + 16


class Plan:

    def __init__(self, stages, counts, straight, pieces):
        self.stages, self.counts, self.straight, self.pieces = stages, counts, straight, pieces

    def piece(self, u):
        return self.pieces.get((u.kind, u.half, u.i), (None, None)) if u.static else (None, None)

    def run(self, engine, kind, half, body):
        beside = [i for k, h, i in self.pieces if (k, h) == (kind, half)]
        looped = (min(beside + [self.straight[kind]]) - 1) // 2
        body(Unit(self, kind, half, 0))
        with engine.Fori(0, looped) as j:
            body(Unit(self, kind, half, 1, j))
            body(Unit(self, kind, half, 2, j))
        for i in range(1 + 2 * looped, self.counts[kind]):
            body(Unit(self, kind, half, i))


def plan_of(heads, chunks, shared_chunks):
    pieces = {}

    def beside(kind, half, start, names, step):
        for n, name in enumerate(names.split()):
            pieces[kind, half, start + n] = (name, step)

    beside("a", 0, heads - 4, "stats norm turn", ("x", 1))
    beside("a", 1, heads - 5, "stats norm squares turn", ("y", 0))
    beside("b", 0, heads - 5, "stats norm squares turn", ("y", 1))
    beside("b", 1, heads - 8, "squares turn logits ranks ties weights spread", ("t", 0))
    beside("m", 0, chunks - 9, "squares turn logits ranks ties weights spread", ("t", 1))
    stages = [(kind, half) for kind in "abm" for half in range(HALVES)]
    return Plan(stages, {"a": heads, "b": heads, "m": chunks},
                {"a": heads - 2, "b": heads - 2, "m": chunks - shared_chunks - 1}, pieces)


def flamingo_layer(nc, x, ctx_t, ctx, head_a, head_b, chunk_m, small, out, shared_units):
    TOK, D = x.shape
    H = head_a.shape[0]
    C = ctx.shape[1]
    CH = chunk_m.shape[0]
    E = 16
    SETUP = 8
    TOP = 6
    WARM_UP = 20
    HT = TOK // HALVES
    NT = HT // P
    KD = D // P
    SPB = P // SEQ
    NS = HT // SEQ
    SCALE = float(P) ** -0.5
    UNITS = 2 * P // E
    GROUPS = 2
    SHARED = -(-shared_units // P)
    assert C == P and D == 2 * P and HT == 512
    AQ, AK, AV, AO = 0, D, 0, C
    A1, A2 = D + P, C + D
    B1, B2 = 3 * D, D
    MG, MU = 0, D
    M1, M2 = 2 * D, D
    SM_GQ, SM_GK, SM_LN1, SM_LN2, SM_GX, SM_GF, SM_GATE = 0, 1, 2, 4, 6, 7, 8
    SM_ID = SM_GATE + KD * E
    SM_MASK = SM_ID + P
    SM_TIE = SM_MASK + SEQ
    SM_W = SM_TIE + E * E

    with ExitStack() as stack:
        def sb(name, shape, dt=F32):
            return stack.enter_context(nc.sbuf_tensor(name, shape, dt))

        def psum(name):
            return stack.enter_context(nc.psum_tensor(name, [P, 512], F32))

        def sem(name):
            return stack.enter_context(nc.semaphore(name))

        sm = sb("sm", [P, SM_W])
        ident = sm[:, SM_ID:SM_ID + P]
        xs = sb("xs", [P, HALVES, NT, D])
        ys = sb("ys", [P, HALVES, NT, D])
        ctx_sb = sb("ctx_sb", [P, HALVES * NT, C])
        ctxt = sb("ctxt", [P, TOK])
        ctxt_hi, ctxt_lo = sb("ctxt_hi", [P, TOK], F32R), sb("ctxt_lo", [P, TOK], F32R)
        xt = sb("xt", [P, KD, HT])
        xt_hi = [sb(f"xt_hi{h}", [P, KD, HT], F32R) for h in range(HALVES)]
        xt_lo = [sb(f"xt_lo{h}", [P, KD, HT], F32R) for h in range(HALVES)]
        hn = sb("hn", [P, NT, D])
        ones, ones_of = sb("ones", [P, 1]), sb("ones_of", [P, SPB, P], F32R)
        zeros = sb("zeros", [P, 512], F32R)
        eps5, eps6 = sb("eps5", [P, 1]), sb("eps6", [P, 1])
        tg = sb("tg", [P, 2])
        gqk = sb("gqk", [P, 1])
        raw_a1 = [sb(f"raw_a1_{p}", [P, A1]) for p in range(2)]
        raw_a2 = [sb(f"raw_a2_{p}", [P, A2]) for p in range(2)]
        raw_b1 = [sb(f"raw_b1_{p}", [P, B1]) for p in range(2)]
        raw_b2 = [sb(f"raw_b2_{p}", [P, B2]) for p in range(2)]
        raw_m1 = [sb(f"raw_m1_{p}", [P, M1]) for p in range(2)]
        raw_m2 = [sb(f"raw_m2_{p}", [P, M2]) for p in range(2)]
        wq_hi, wq_lo = sb("wq_hi", [P, D], F32R), sb("wq_lo", [P, D], F32R)
        wk_hi, wk_lo = sb("wk_hi", [P, D], F32R), sb("wk_lo", [P, D], F32R)
        wv_hi, wv_lo = sb("wv_hi", [P, D], F32R), sb("wv_lo", [P, D], F32R)
        wo_hi, wo_lo = sb("wo_hi", [P, D], F32R), sb("wo_lo", [P, D], F32R)
        vo_hi, vo_lo = sb("vo_hi", [P, H, D], F32R), sb("vo_lo", [P, H, D], F32R)
        sq_q, sq_k = sb("sq_q", [P, HT]), sb("sq_k", [P, HT])
        sq_k_hi, sq_k_lo = sb("sq_k_hi", [P, HT], F32R), sb("sq_k_lo", [P, HT], F32R)
        qt, kt, vt = sb("qt", [P, HT]), sb("kt", [P, HT]), sb("vt", [P, HT])
        vs = sb("vs", [P, NT, P])
        ln_k, ln_q = sb("ln_k", [P, NT, SEQ]), sb("ln_q", [P, NT])
        ln_qk, r_qk = sb("ln_qk", [P, NT, SEQ]), sb("r_qk", [P, NT, SEQ])
        sc = sb("sc", [P, NT, SEQ])
        sc_max = sb("sc_max", [P, NT])
        sc_sub = sb("sc_sub", [P, NT, SEQ])
        ex = sb("ex", [P, NT, SEQ])
        ex_sum, ex_inv = sb("ex_sum", [P, NT]), sb("ex_inv", [P, NT])
        attn = sb("attn", [P, NT, P])
        attn_t = sb("attn_t", [P, HT])
        pv_hi, pv_lo = sb("pv_hi", [P, HT], F32R), sb("pv_lo", [P, HT], F32R)
        gs, gu, hh = sb("gs", [P, HT]), sb("gu", [P, HT]), sb("hh", [P, HT])
        unit_w = [sb(f"unit_w{h}", [P, GROUPS, HT]) for h in range(HALVES)]
        bn = sb("bn", [P, NT, 6])
        mv = sb("mv", [P, NT, 2])
        ms = sb("ms", [P, NT])
        st = sb("st", [P, 8, NT])
        junk = sb("junk", [P, D])
        rt = sb("rt", [P, 6, NT, E])
        rmax = sb("rmax", [P, 4, NT])
        pair1, pair2 = sb("pair1", [P, NT, E, E]), sb("pair2", [P, NT, E, E])
        cw = sb("cw", [P, NT, E, UNITS])

        acc = [psum("acc0"), psum("acc1")]
        bank_q, bank_k, bank_v = psum("bank_q"), psum("bank_k"), psum("bank_v")
        bank_s, bank_t, bank_p = psum("bank_s"), psum("bank_t"), psum("bank_p")

        ld_small, ld_ctx = sem("ld_small"), sem("ld_ctx")
        ld_ctxt = [sem(f"ld_ctxt{h}") for h in range(HALVES)]
        ld_x = [[sem(f"ld_x{h}_{t}") for t in range(NT)] for h in range(HALVES)]
        ld_a1 = [sem(f"ld_a1_{p}") for p in range(2)]
        ld_a2 = [sem(f"ld_a2_{p}") for p in range(2)]
        ld_b1 = [sem(f"ld_b1_{p}") for p in range(2)]
        ld_b2 = [sem(f"ld_b2_{p}") for p in range(2)]
        ld_m1 = [sem(f"ld_m1_{p}") for p in range(2)]
        ld_m2 = [sem(f"ld_m2_{p}") for p in range(2)]
        st_out = sem("st_out")

        def stage_sems(tag, names):
            return {n: sem(f"{tag}_{n}") for n in names.split()}

        A = stage_sems("a", "wq_hi wq_lo wk_hi wk_lo q_done k_done sq_q sq_k sq_k_hi sq_k_lo qt kt scores scaled max "
                       "sub exp sum inv norm_lo norm_hi t_done attn_t vo_done vo_hi vo_lo ssk_done ssq_done ln_q "
                       "ln_k ln_qk r_qk pv_done pv_hi pv_lo wo_done")
        B = stage_sems("b", "wq_hi wq_lo wk_hi wk_lo wv_hi wv_lo wo_hi wo_lo q_done k_done v_done qt kt vt "
                       "vtr_done vs scores scaled max sub exp sum inv norm_lo norm_hi t_done attn_t "
                       "pv_done pv_hi pv_lo wo_done")
        M = stage_sems("m", "wg_hi wg_lo wu_hi wu_lo wd_hi wd_lo g_done u_done silu weighted hh hh_hi hh_lo down")

        dve, act = Counter(sem("dve_step")), Counter(sem("act_step"))
        pe_tr = sem("pe_tr")
        pe_gate = sem("pe_gate")
        pe_cw = sem("pe_cw")
        tok_ready = sem("tok_ready")
        cw_ready = sem("cw_ready")
        var_ready, rough = sem("var_ready"), sem("rough")
        y_ready = sem("y_ready")
        xt_ready, xt_hi_ready, xt_lo_ready = sem("xt_ready"), sem("xt_hi_ready"), sem("xt_lo_ready")
        logits_sub, logits_exp = sem("logits_sub"), sem("logits_exp")
        unit_w_ready = sem("unit_w_ready")
        acc_free = sem("acc_free")
        setup_pool, setup_dve, setup_act = sem("setup_pool"), sem("setup_dve"), sem("setup_act")
        ctxt_hi_ready, ctxt_lo_ready = sem("ctxt_hi_ready"), sem("ctxt_lo_ready")
        out_ready = sem("out_ready")

        def tiles(ap):
            return ap.rearrange("p (t n) -> p t n", t=NT)

        stages = {"a": A, "b": B, "m": M}
        plan = plan_of(H, CH, SHARED)
        STAGES = plan.stages
        PREP = {(step, half): n for n, (step, half) in enumerate((s_, h_) for s_ in "xyt" for h_ in range(HALVES))}
        piece_at, run_units = plan.piece, plan.run

        def first_unit(kind, half):
            return Unit(plan, kind, half, 0)

        def turn_banks(u):
            return (bank_p, bank_t if u.kind == "m" else bank_v)

        def gate_bank(u):
            return (bank_q, bank_v)[u.parity]

        def up_bank(u):
            return (bank_k, bank_s)[u.parity]

        block = stack.enter_context(nc.Block())

        @block.sync
        def _(sp):
            x_v = x.rearrange("(h t p) d -> h p t d", h=HALVES, p=P)
            out_v = out.rearrange("(h t p) d -> h p t d", h=HALVES, p=P)

            def load_a1(u):
                sp.dma_start(raw_a1[u.parity][:], head_a[bass.ds(u.i, 1), :, 0:A1].rearrange("h p n -> p (h n)")).then_inc(ld_a1[u.parity], 16)

            def load_a2(u):
                sp.dma_start(raw_a2[u.parity][:], head_a[bass.ds(u.i, 1), :, A1:A1 + A2].rearrange("h p n -> p (h n)")).then_inc(ld_a2[u.parity], 16)

            def load_b1(u):
                sp.dma_start(raw_b1[u.parity][:], head_b[bass.ds(u.i, 1), :, 0:B1].rearrange("h p n -> p (h n)")).then_inc(ld_b1[u.parity], 16)

            def load_b2(u):
                sp.dma_start(raw_b2[u.parity][:], head_b[bass.ds(u.i, 1), :, B1:B1 + B2].rearrange("h p n -> p (h n)")).then_inc(ld_b2[u.parity], 16)

            def load_m1(u):
                sp.dma_start(raw_m1[u.parity][:], chunk_m[bass.ds(u.i, 1), :, 0:M1].rearrange("h p n -> p (h n)")).then_inc(ld_m1[u.parity], 16)

            def load_m2(u):
                sp.dma_start(raw_m2[u.parity][:], chunk_m[bass.ds(u.i, 1), :, M1:M1 + M2].rearrange("h p n -> p (h n)")).then_inc(ld_m2[u.parity], 16)

            def load_x(half):
                for t in range(NT):
                    sp.dma_start(xs[:, half, t], x_v[half, :, t]).then_inc(ld_x[half][t], 16)

            load_x(0)
            sp.dma_start(sm[:], small).then_inc(ld_small, 16)
            load_a1(first_unit("a", 0))
            sp.dma_start(ctxt[:, 0:HT], ctx_t[:, 0:HT]).then_inc(ld_ctxt[0], 16)
            load_a1(first_unit("a", 0).next())
            load_a2(first_unit("a", 0))
            sp.dma_start(ctx_sb[:], ctx.rearrange("(t p) c -> p t c", p=P)).then_inc(ld_ctx, 16)
            load_a2(first_unit("a", 0).next())
            sp.dma_start(ctxt[:, HT:TOK], ctx_t[:, HT:TOK]).then_inc(ld_ctxt[1], 16)
            load_x(1)
            for i in range(2):
                load_b1(Unit(plan, "b", 0, i))
                load_b2(Unit(plan, "b", 0, i))
                load_m1(Unit(plan, "m", 0, i))
                load_m2(Unit(plan, "m", 0, i))

            def refill(kind, half, loads):
                def unit(u):
                    for load, users in loads:
                        for user in users:
                            sp.wait_ge(user, u.done(2))
                        load(u)
                count = plan.counts[kind]
                start = 0 if half else 2
                pairs = (count - start) // 2
                with sp.Fori(0, pairs) as j:
                    unit(Unit(plan, kind, half, start, j))
                    unit(Unit(plan, kind, half, start + 1, j))
                if (count - start) % 2:
                    unit(Unit(plan, kind, half, count - 1))

            refill("a", 0, [(load_a1, (A["wq_lo"], A["wk_lo"])), (load_a2, (A["vo_done"],))])
            refill("a", 1, [(load_a1, (A["wq_lo"], A["wk_lo"]))])
            for half in range(HALVES):
                refill("b", half, [(load_b1, (B["wq_lo"], B["wk_lo"], B["wv_lo"])), (load_b2, (B["wo_lo"],))])
            for half in range(HALVES):
                refill("m", half, [(load_m1, (M["wg_lo"], M["wu_lo"])), (load_m2, (M["wd_lo"],))])
            for half in range(HALVES):
                sp.wait_ge(out_ready, half + 1)
                sp.dma_start(out_v[half], xs[:, half]).then_inc(st_out, 16)
            sp.wait_ge(st_out, 16 * HALVES)

        @block.tensor
        def _(pe):
            def project(bank, w_hi, w_lo, m_hi, m_lo, chunks=KD):
                n = 0
                for k in range(chunks):
                    cols = slice(k * P, (k + 1) * P)
                    for w, m in ((w_hi, m_hi), (w_hi, m_lo), (w_lo, m_hi)):
                        last = nc.tensor.matmul(bank[:], w[:, cols], m(k), start=n == 0, stop=n == 3 * chunks - 1)
                        n += 1
                return last

            def tokens_hi(u):
                return lambda k: xt_hi[u.half][:, k, :]

            def tokens_lo(u):
                return lambda k: xt_lo[u.half][:, k, :]

            def clear_acc(u):
                if u.stage_number:
                    pe.wait_ge(acc_free, u.stage_number)
                for bank in acc:
                    last = nc.tensor.matmul(bank[:], zeros[:, 0:P], zeros[:], start=True, stop=True, skip_group_check=True)

            def output(u):
                if u.kind == "a":
                    pe.wait_ge(A["pv_lo"], u.done())
                    if u.half == 0:
                        pe.wait_ge(A["vo_lo"], u.done())
                    w_hi, w_lo = vo_hi[:, bass.ds(u.i, 1), :].squeeze(1), vo_lo[:, bass.ds(u.i, 1), :].squeeze(1)
                    done = A["wo_done"]
                elif u.kind == "b":
                    pe.wait_ge(B["pv_lo"], u.done())
                    pe.wait_ge(B["wo_lo"], u.done())
                    w_hi, w_lo = wo_hi[:], wo_lo[:]
                    done = B["wo_done"]
                else:
                    pe.wait_ge(M["hh_lo"], u.done())
                    pe.wait_ge(M["wd_lo"], u.done())
                    w_hi, w_lo = wo_hi[:], wo_lo[:]
                    done = M["down"]
                for t in range(NT):
                    tok = slice(t * P, (t + 1) * P)
                    for w, m in ((pv_hi, w_hi), (pv_hi, w_lo), (pv_lo, w_hi)):
                        last = nc.tensor.matmul(acc[t // 2][:, (t % 2) * D:(t % 2 + 1) * D], w[:, tok], m,
                                                start=False, stop=True, skip_group_check=True)
                last.then_inc(done, 1)

            def project_first(u):
                if u.needs_tokens:
                    pe.wait_ge(xt_lo_ready, u.tokens_number)
                if u.kind == "a":
                    pe.wait_ge(A["wq_lo"], u.done())
                    project(bank_q, wq_hi, wq_lo, tokens_hi(u), tokens_lo(u)).then_inc(A["q_done"], 1)
                elif u.kind == "b":
                    pe.wait_ge(B["wq_lo"], u.done())
                    project(bank_q, wq_hi, wq_lo, tokens_hi(u), tokens_lo(u)).then_inc(B["q_done"], 1)
                else:
                    if not u.in_first_pair:
                        pe.wait_ge(M["silu"], u.done(2))
                    pe.wait_ge(M["wg_lo"], u.done())
                    project(gate_bank(u), wq_hi, wq_lo, tokens_hi(u), tokens_lo(u)).then_inc(M["g_done"], 1)
                    if not u.in_first_pair:
                        pe.wait_ge(M["hh"], u.done(2))
                    pe.wait_ge(M["wu_lo"], u.done())
                    project(up_bank(u), wk_hi, wk_lo, tokens_hi(u), tokens_lo(u)).then_inc(M["u_done"], 1)

            def project_keys(u):
                if u.kind == "a":
                    pe.wait_ge(A["wk_lo"], u.done())
                    if u.needs_tokens:
                        pe.wait_ge(ctxt_lo_ready, u.half + 1)
                    toks = slice(u.half * HT, (u.half + 1) * HT)
                    project(bank_k, wk_hi, wk_lo, lambda k: ctxt_hi[:, toks], lambda k: ctxt_lo[:, toks], 1)\
                        .then_inc(A["k_done"], 1)
                elif u.kind == "b":
                    pe.wait_ge(B["wk_lo"], u.done())
                    project(bank_k, wk_hi, wk_lo, tokens_hi(u), tokens_lo(u)).then_inc(B["k_done"], 1)

            def project_values(u):
                pe.wait_ge(B["wv_lo"], u.done())
                project(bank_v, wv_hi, wv_lo, tokens_hi(u), tokens_lo(u)).then_inc(B["v_done"], 1)

            def turn_values(u):
                pe.wait_ge(B["vt"], u.done())
                for t in range(NT):
                    last = nc.tensor.transpose(bank_t[:, t * P:(t + 1) * P], vt[:, t * P:(t + 1) * P], ident)
                last.then_inc(B["vtr_done"], 1)

            def value_out(u):
                pe.wait_ge(ld_a2[u.parity], u.loads())
                nc.tensor.matmul(bank_v[:, 0:D], raw_a2[u.parity][:, AV:AV + C], raw_a2[u.parity][:, AO:AO + D],
                                 start=True, stop=True).then_inc(A["vo_done"], 1)

            def norm_q(u):
                pe.wait_ge(A["sq_q"], u.done())
                for t in range(NT):
                    last = nc.tensor.matmul(bank_s[:, NT * SEQ + t:NT * SEQ + t + 1], sq_q[:, t * P:(t + 1) * P], ones[:],
                                            start=True, stop=True)
                last.then_inc(A["ssq_done"], 1)

            def norm_k(u):
                pe.wait_ge(A["sq_k_lo"], u.done())
                for s in range(SPB):
                    for part, square in enumerate((sq_k_hi, sq_k_lo)):
                        keys = square[:].rearrange("p (t s k) -> p t s k", s=SPB, k=SEQ)[:, :, s, :]
                        first, final = s + part == 0, s + part == SPB
                        last = nc.tensor.matmul(bank_v[:, D:D + NT * SEQ], ones_of[:, s, :], keys,
                                                start=first, stop=final)
                last.then_inc(A["ssk_done"], 1)

            def scores(u):
                stage = stages[u.kind]
                pe.wait_ge(stage["qt"], u.done())
                pe.wait_ge(stage["kt"], u.done())
                if u.kind == "a":
                    pe.wait_ge(A["ln_q"], u.done())
                for b in range(NS):
                    tok = slice(b * SEQ, (b + 1) * SEQ)
                    t, s = b // SPB, b % SPB
                    last = nc.tensor.matmul(bank_s[s * SEQ:(s + 1) * SEQ, t * SEQ:(t + 1) * SEQ], qt[:, tok], kt[:, tok],
                                            start=True, stop=True)
                last.then_inc(stage["scores"], 1)

            def turn_attn(u):
                stage = stages[u.kind]
                pe.wait_ge(stage["norm_hi"], u.done())
                if u.kind == "b":
                    pe.wait_ge(B["vs"], u.done())
                for t in range(NT):
                    last = nc.tensor.transpose(bank_t[:, t * P:(t + 1) * P], attn[:, t, :], ident)
                last.then_inc(stage["t_done"], 1)

            def attn_values(u):
                stage = stages[u.kind]
                if u.kind == "a" and u.very_first:
                    pe.wait_ge(ld_ctx, 16)
                pe.wait_ge(stage["attn_t"], u.done())
                for t in range(NT):
                    value = ctx_sb[:, u.half * NT + t, :] if u.kind == "a" else vs[:, t, :]
                    last = nc.tensor.matmul(bank_p[:, t * P:(t + 1) * P], value, attn_t[:, t * P:(t + 1) * P],
                                            start=True, stop=True)
                last.then_inc(stage["pv_done"], 1)

            def turn_tokens(step, banks):
                pe.wait_ge(tok_ready, PREP[step] + 1)
                for k, bank in enumerate(banks):
                    for t in range(NT):
                        last = nc.tensor.transpose(bank[:, t * P:(t + 1) * P], hn[:, t, k * P:(k + 1) * P], ident)
                last.then_inc(pe_tr, 1)

            def prepare(u):
                piece, step = piece_at(u)
                if piece == "turn":
                    turn_tokens(step, turn_banks(u))
                    return [(xt_lo_ready, PREP[step] + 1)]
                if piece == "logits":
                    pe.wait_ge(xt_ready, step[1] + 1)
                    pe.wait_ge(xt_lo_ready, PREP[step] + 1)
                    for t in range(NT):
                        for k in range(KD):
                            last = nc.tensor.matmul(bank_p[:, t * E:(t + 1) * E], xt[:, k, t * P:(t + 1) * P],
                                                    sm[:, SM_GATE + k * E:SM_GATE + (k + 1) * E],
                                                    start=k == 0, stop=k == KD - 1)
                    last.then_inc(pe_gate, 1)
                    return [(logits_sub, step[1] + 1)]
                if piece == "spread":
                    pe.wait_ge(cw_ready, step[1] + 1)
                    for g, bank in enumerate(turn_banks(u)):
                        experts = slice(g * E // GROUPS, (g + 1) * E // GROUPS)
                        for t in range(NT):
                            last = nc.tensor.transpose(bank[:, t * P:(t + 1) * P],
                                                       cw[:, t, experts, :].rearrange("p e n -> p (e n)"), ident)
                    last.then_inc(pe_cw, 1)
                    return [(unit_w_ready, step[1] + 1)]
                return []

            def head(u):
                prev, nxt = u.prev(), u.next()

                def small_products():
                    if u.kind == "a" and u.half == 0:
                        value_out(u)
                    if nxt.kind == "a":
                        pe.wait_ge(A["scaled"], u.done())
                        norm_q(nxt)
                        norm_k(nxt)

                scores(u)
                if prev and prev.deferred:
                    attn_values(prev)
                if nxt.kind == "a":
                    project_keys(nxt)
                project_first(nxt)
                if prev:
                    output(prev)
                if u.kind == "a":
                    pe.wait_ge(A["ln_k"], u.done())
                held = prepare(u)
                if nxt.kind == "b":
                    project_keys(nxt)
                if not held:
                    small_products()
                turn_attn(u)
                for semaphore, value in held:
                    pe.wait_ge(semaphore, value)
                if held:
                    small_products()
                if nxt.kind == "b":
                    project_values(nxt)
                if not u.deferred:
                    attn_values(u)
                if nxt.kind == "b":
                    turn_values(nxt)
                if u.first:
                    clear_acc(u)

            def chunk(u):
                prev, nxt = u.prev(), u.next()
                if u.very_first:
                    output(prev)
                if nxt:
                    project_first(nxt)
                prepare(u)
                if u.first:
                    clear_acc(u)
                output(u)

            pe.wait_ge(setup_pool, SETUP)
            for _ in range(WARM_UP):
                nc.tensor.matmul(bank_s[:], zeros[:, 0:P], zeros[:], start=True, stop=True)
            pe.wait_ge(ld_small, 16)
            start = first_unit("a", 0)
            project_keys(start)
            turn_tokens(("x", 0), (bank_p, bank_t))
            for _ in range(WARM_UP // 2):
                nc.tensor.matmul(bank_s[:], zeros[:, 0:P], zeros[:], start=True, stop=True)
            project_first(start)
            norm_q(start)
            norm_k(start)
            for kind, half in STAGES:
                run_units(pe, kind, half, chunk if kind == "m" else head)

        @block.scalar
        def _(act_e):
            def rough_root(step):
                act_e.wait_ge(var_ready, PREP[step] + 1)
                act.link(act_e, nc.scalar.activation(st[:, 1, :], st[:, 0, :], ACT.Ln))
                nc.scalar.activation(st[:, 1, :], st[:, 1, :], ACT.Exp, scale=-0.5).then_inc(rough, 1)

            def mean_squares(source):
                for t in range(NT):
                    act.link(act_e, nc.scalar.activation(junk[:], source[:, t, :], ACT.Square, scale=float(D) ** -0.5,
                                                         accum_out=ms[:, t:t + 1]))
                act.link(act_e, nc.scalar.activation(st[:, 1, :], ms[:], ACT.Ln, bias=eps6[:, 0:1]))
                nc.scalar.activation(st[:, 1, :], st[:, 1, :], ACT.Exp, scale=-0.5).then_inc(rough, 1)

            def take_tokens(step, banks):
                kind, half = step
                act_e.wait_ge(pe_tr, PREP[step] + 1)
                if kind == "t" and half:
                    act_e.wait_ge(pe_gate, half)
                for k, bank in enumerate(banks):
                    def take(target):
                        if kind == "x":
                            return nc.scalar.activation(target[:, k, :], bank[:], ACT.Copy)
                        col = (SM_LN1 if kind == "y" else SM_LN2) + k
                        return nc.scalar.activation(target[:, k, :], bank[:], ACT.Identity, scale=sm[:, col:col + 1])
                    if kind == "t":
                        last = take(xt)
                    take(xt_hi[half]).then_inc(xt_hi_ready, 1)
                if kind == "t":
                    last.then_inc(xt_ready, 1)

            def prepare(u):
                piece, step = piece_at(u)
                if piece == "norm":
                    rough_root(step)
                if piece == "squares":
                    if u.kind == "m":
                        act_e.preload_act_table_set(LN_EXP)
                    if step[0] == "y":
                        act_e.wait_ge(y_ready, step[1] + 1)
                    else:
                        act_e.wait_ge(acc_free, STAGES.index(("b", step[1])) + 1)
                    mean_squares(ys[:, step[1]])
                if piece == "turn":
                    take_tokens(step, turn_banks(u))
                if piece == "ranks":
                    act_e.wait_ge(logits_sub, step[1] + 1)
                    nc.scalar.activation(rt[:, 1], rt[:, 0], ACT.Exp).then_inc(logits_exp, 1)
                if piece == "spread":
                    act_e.wait_ge(pe_cw, step[1] + 1)
                    for g, bank in enumerate(turn_banks(u)):
                        last = nc.scalar.activation(unit_w[step[1]][:, g, :], bank[:], ACT.Copy)
                    last.then_inc(unit_w_ready, 1)

            def square_q(u):
                act_e.wait_ge(A["q_done"], u.done())
                nc.scalar.activation(sq_q[:], bank_q[:], ACT.Square, scale=SCALE).then_inc(A["sq_q"], 1)

            def square_k(u):
                act_e.wait_ge(A["k_done"], u.done())
                nc.scalar.activation(sq_k[:], bank_k[:], ACT.Square, scale=SCALE).then_inc(A["sq_k"], 1)
                nc.scalar.activation(sq_k_hi[:], bank_k[:], ACT.Square, scale=SCALE).then_inc(A["sq_k_hi"], 1)

            def take_k(u):
                if u.kind == "a":
                    nc.scalar.activation(kt[:], bank_k[:], ACT.Identity, scale=gqk[:, 0:1]).then_inc(A["kt"], 1)
                if u.kind == "b":
                    act_e.wait_ge(B["k_done"], u.done())
                    nc.scalar.activation(kt[:], bank_k[:], ACT.Copy).then_inc(B["kt"], 1)

            def take_v(u):
                act_e.wait_ge(B["v_done"], u.done())
                nc.scalar.activation(vt[:], bank_v[:], ACT.Copy).then_inc(B["vt"], 1)

            def log_q(u):
                act_e.wait_ge(A["ssq_done"], u.done())
                nc.scalar.activation(ln_q[:], bank_s[:, NT * SEQ:NT * SEQ + NT], ACT.Ln, bias=eps5[:, 0:1]).then_inc(A["ln_q"], 1)

            def log_k(u):
                act_e.wait_ge(A["ssk_done"], u.done())
                nc.scalar.activation(ln_k[:], tiles(bank_v[:, D:D + NT * SEQ]), ACT.Ln, bias=eps5[:, 0:1])\
                    .then_inc(A["ln_k"], 1)

            def roots(u):
                act_e.wait_ge(A["ln_qk"], u.done())
                nc.scalar.activation(r_qk[:], ln_qk[:], ACT.Exp, scale=-0.5).then_inc(A["r_qk"], 1)

            def take_values(u):
                stage = stages[u.kind]
                act_e.wait_ge(stage["pv_done"], u.done())
                nc.scalar.activation(pv_hi[:], bank_p[:], ACT.Copy).then_inc(stage["pv_hi"], 1)

            def gate(u):
                act_e.wait_ge(M["g_done"], u.done())
                if not u.very_first:
                    act_e.wait_ge(M["weighted"], u.done(1))
                nc.scalar.activation(gs[:], gate_bank(u)[:], ACT.Silu).then_inc(M["silu"], 1)

            def split_hidden(u):
                act_e.wait_ge(M["hh"], u.done())
                if u.very_first:
                    act_e.wait_ge(B["wo_done"], u.prev().done())
                else:
                    act_e.wait_ge(M["down"], u.done(1))
                nc.scalar.activation(pv_hi[:], hh[:], ACT.Copy).then_inc(M["hh_hi"], 1)

            def head(u):
                stage, nxt = stages[u.kind], u.next()
                turning = piece_at(u)[0] == "turn"
                if u.prev() and u.prev().deferred:
                    take_values(u.prev())
                if nxt.kind == "a":
                    square_k(nxt)
                act_e.wait_ge(stage["sub"], u.done())
                nc.scalar.activation(ex[:], sc_sub[:], ACT.Exp).then_inc(stage["exp"], 1)
                if nxt.kind == "a":
                    square_q(nxt)
                if nxt.kind == "m":
                    gate(nxt)
                prepare(u)
                take_k(nxt)
                if nxt.kind == "a" and not turning:
                    log_q(nxt)
                    log_k(nxt)
                act_e.wait_ge(stage["t_done"], u.done())
                nc.scalar.activation(attn_t[:], bank_t[:], ACT.Copy).then_inc(stage["attn_t"], 1)
                if nxt.kind == "a" and turning:
                    log_q(nxt)
                    log_k(nxt)
                if u.kind == "a" and u.half == 0:
                    act_e.wait_ge(A["vo_done"], u.done())
                    nc.scalar.activation(vo_hi[:, bass.ds(u.i, 1), :].squeeze(1), bank_v[:, 0:D], ACT.Copy)\
                        .then_inc(A["vo_hi"], 1)
                if nxt.kind == "b":
                    take_v(nxt)
                if not u.deferred:
                    take_values(u)
                if nxt.kind == "a":
                    roots(nxt)

            def chunk(u):
                nxt = u.next()
                if u.very_first:
                    split_hidden(u)
                if nxt:
                    gate(nxt)
                prepare(u)
                if nxt:
                    split_hidden(nxt)

            def split_context(half):
                act_e.wait_ge(ld_ctxt[half], 16)
                toks = slice(half * HT, (half + 1) * HT)
                nc.scalar.activation(ctxt_hi[:, toks], ctxt[:, toks], ACT.Copy).then_inc(ctxt_hi_ready, 1)

            act_e.wait_ge(ld_small, 16)
            nc.scalar.activation(tg[:], sm[:, SM_GX:SM_GF + 1], ACT.Tanh).then_inc(setup_act, 1)
            act_e.preload_act_table_set(LN_EXP)
            split_context(0)
            act_e.wait_ge(setup_dve, 1)
            act_e.wait_ge(setup_pool, SETUP)
            rough_root(("x", 0))
            start = first_unit("a", 0)
            square_k(start)
            take_k(start)
            take_tokens(("x", 0), (bank_p, bank_t))
            square_q(start)
            split_context(1)
            log_q(start)
            log_k(start)
            roots(start)
            for kind, half in STAGES:
                run_units(act_e, kind, half, chunk if kind == "m" else head)

        @block.vector
        def _(v):
            def link(ins):
                dve.link(v, ins)

            roots_taken = Counter(rough)

            def await_root():
                roots_taken.n += 1
                v.wait_ge(rough, roots_taken.n)

            def refined_root():
                link(nc.vector.tensor_tensor(st[:, 3, :], st[:, 0, :], st[:, 1, :], ALU.mult))
                link(nc.vector.tensor_tensor(st[:, 4, :], st[:, 3, :], st[:, 1, :], ALU.mult))
                link(nc.vector.tensor_scalar(st[:, 5, :], st[:, 4, :], -0.5, 1.5, ALU.mult, ALU.add))
                link(nc.vector.tensor_tensor(st[:, 2, :], st[:, 1, :], st[:, 5, :], ALU.mult))

            def per_expert(ap):
                return ap.unsqueeze(2).to_broadcast([P, NT, E])

            mine = rt[:, 2].unsqueeze(3).to_broadcast([P, NT, E, E])
            others = rt[:, 2].unsqueeze(2).to_broadcast([P, NT, E, E])

            def prepare_piece(piece, step, u=None):
                if not piece:
                    return
                kind, half = step
                if piece == "stats":
                    for t in range(NT):
                        if kind == "x":
                            v.wait_ge(ld_x[half][t], 16)
                        dve.mark(nc.vector.bn_stats(bn[:, t, :], xs[:, half, t, :]))
                    v.wait_ge(dve.sem, dve.n)
                    for t in range(NT):
                        dve.mark(nc.vector.bn_aggr(mv[:, t, :], bn[:, t, :]))
                    v.wait_ge(dve.sem, dve.n)
                    nc.vector.tensor_scalar(st[:, 0, :], mv[:, :, 1], 1e-5, None, ALU.add).then_inc(var_ready, 1)
                if piece == "norm":
                    await_root()
                    refined_root()
                    target, signal = (hn[:], tok_ready) if kind == "x" else (ys[:, half], y_ready)
                    if kind == "x" and PREP[step]:
                        v.wait_ge(pe_tr, PREP[step])
                    for t in range(NT):
                        last = nc.vector.tensor_scalar(target[:, t, :], xs[:, half, t, :], mv[:, t, 0:1],
                                                       st[:, 2, t:t + 1], ALU.subtract, ALU.mult)
                    last.then_inc(signal, 1)
                if piece == "squares":
                    await_root()
                    link(nc.vector.tensor_scalar(st[:, 0, :], ms[:], 1e-6, None, ALU.add))
                    refined_root()
                    v.wait_ge(pe_tr, PREP[step])
                    for t in range(NT):
                        last = nc.vector.tensor_scalar(hn[:, t, :], ys[:, half, t, :], st[:, 2, t:t + 1], None, ALU.mult)
                    last.then_inc(tok_ready, 1)
                if piece == "turn":
                    for k, bank in enumerate(turn_banks(u) if u else (bank_p, bank_t)):
                        v.wait_ge(xt_hi_ready, KD * PREP[step] + k + 1)
                        if kind == "x":
                            last = nc.vector.tensor_tensor(xt_lo[half][:, k, :], bank[:], xt_hi[half][:, k, :],
                                                           ALU.subtract)
                        else:
                            col = (SM_LN1 if kind == "y" else SM_LN2) + k
                            last = nc.vector.scalar_tensor_tensor(xt_lo[half][:, k, :], bank[:], sm[:, col:col + 1],
                                                                  xt_hi[half][:, k, :], ALU.mult, ALU.subtract)
                    last.then_inc(xt_lo_ready, 1)
                if piece == "logits":
                    v.wait_ge(pe_gate, half + 1)
                    logits = bank_p[:, 0:NT * E].rearrange("p (t e) -> p t e", e=E)
                    link(nc.vector.tensor_reduce(rmax[:, 0, :], logits, AX, ALU.max))
                    nc.vector.tensor_tensor(rt[:, 0], logits, per_expert(rmax[:, 0, :]), ALU.subtract).then_inc(logits_sub, 1)
                if piece == "ranks":
                    v.wait_ge(logits_exp, half + 1)
                    link(nc.vector.tensor_reduce(rmax[:, 1, :], rt[:, 1], AX, ALU.add))
                    link(nc.vector.reciprocal(rmax[:, 2, :], rmax[:, 1, :]))
                    link(nc.vector.tensor_tensor(rt[:, 2], rt[:, 1], per_expert(rmax[:, 2, :]), ALU.mult))
                    link(nc.vector.tensor_tensor(pair1[:], others, mine, ALU.is_equal))
                if piece == "ties":
                    tie = sm[:, SM_TIE:SM_TIE + E * E].rearrange("p (e f) -> p e f", f=E).unsqueeze(1)
                    link(nc.vector.tensor_tensor(pair1[:], pair1[:], tie.to_broadcast([P, NT, E, E]), ALU.mult))
                    link(nc.vector.tensor_tensor(pair2[:], others, mine, ALU.is_gt))
                if piece == "weights":
                    link(nc.vector.tensor_tensor(pair1[:], pair1[:], pair2[:], ALU.add))
                    link(nc.vector.tensor_reduce(rt[:, 3], pair1[:], AX, ALU.add))
                    link(nc.vector.tensor_scalar(rt[:, 4], rt[:, 3], float(TOP), None, ALU.is_lt))
                    link(nc.vector.tensor_tensor(rt[:, 5], rt[:, 4], rt[:, 2], ALU.mult))
                    link(nc.vector.tensor_reduce(rmax[:, 3, :], rt[:, 5], AX, ALU.add))
                    link(nc.vector.reciprocal(rmax[:, 1, :], rmax[:, 3, :]))
                    nc.vector.tensor_tensor(cw[:], rt[:, 5].unsqueeze(3).to_broadcast([P, NT, E, UNITS]),
                                            per_expert(rmax[:, 1, :]).unsqueeze(3).to_broadcast([P, NT, E, UNITS]),
                                            ALU.mult).then_inc(cw_ready, 1)

            def split_pv(u):
                stage = stages[u.kind]
                v.wait_ge(stage["pv_hi"], u.done())
                nc.vector.tensor_tensor(pv_lo[:], bank_p[:], pv_hi[:], ALU.subtract).then_inc(stage["pv_lo"], 1)

            def softmax(u):
                stage = stages[u.kind]
                if u.kind == "a":
                    v.wait_ge(A["r_qk"], u.done())
                v.wait_ge(stage["scores"], u.done())
                found = tiles(bank_s[:, 0:NT * SEQ])
                if u.kind == "a":
                    nc.vector.tensor_tensor(sc[:], found, r_qk[:], ALU.mult).then_inc(A["scaled"], 1)
                else:
                    mask = sm[:, SM_MASK:SM_MASK + SEQ].unsqueeze(1).to_broadcast([P, NT, SEQ])
                    nc.vector.scalar_tensor_tensor(sc[:], found, SCALE, mask, ALU.mult, ALU.add).then_inc(B["scaled"], 1)
                v.wait_ge(stage["scaled"], u.done())
                nc.vector.tensor_reduce(sc_max[:], sc[:], AX, ALU.max).then_inc(stage["max"], 1)
                v.wait_ge(stage["max"], u.done())
                nc.vector.tensor_tensor(sc_sub[:], sc[:], sc_max[:].unsqueeze(2).to_broadcast([P, NT, SEQ]),
                                        ALU.subtract).then_inc(stage["sub"], 1)
                if u.prev() and u.prev().deferred:
                    split_pv(u.prev())
                v.wait_ge(stage["exp"], u.done())
                nc.vector.tensor_reduce(ex_sum[:], ex[:], AX, ALU.add).then_inc(stage["sum"], 1)
                v.wait_ge(stage["sum"], u.done())
                nc.vector.reciprocal(ex_inv[:], ex_sum[:]).then_inc(stage["inv"], 1)
                v.wait_ge(stage["inv"], u.done())
                for s, signal in ((0, stage["norm_lo"]), (1, stage["norm_hi"])):
                    rows = slice(s * SEQ, (s + 1) * SEQ)
                    nc.vector.tensor_tensor(attn[rows, :, s * SEQ:(s + 1) * SEQ], ex[rows],
                                            ex_inv[rows].unsqueeze(2).to_broadcast([SEQ, NT, SEQ]), ALU.mult)\
                        .then_inc(signal, 1)

            def take_q(u):
                if u.kind == "a":
                    v.wait_ge(A["sq_q"], u.done())
                    nc.vector.tensor_copy(qt[:], bank_q[:]).then_inc(A["qt"], 1)
                if u.kind == "b":
                    v.wait_ge(B["q_done"], u.done())
                    nc.vector.tensor_copy(qt[:], bank_q[:]).then_inc(B["qt"], 1)

            def split_first(u, user):
                if user:
                    v.wait_ge(M["g_done"] if user.kind == "m" else stages[user.kind]["q_done"], user.done())
                if u.kind == "a":
                    v.wait_ge(ld_a1[u.parity], u.loads())
                    nc.vector.tensor_copy(wq_hi[:], raw_a1[u.parity][:, AQ:AQ + D]).then_inc(A["wq_hi"], 1)
                elif u.kind == "b":
                    v.wait_ge(ld_b1[u.parity], u.loads())
                    nc.vector.tensor_copy(wq_hi[:], raw_b1[u.parity][:, 0:D]).then_inc(B["wq_hi"], 1)
                else:
                    v.wait_ge(ld_m1[u.parity], u.loads())
                    nc.vector.tensor_copy(wq_hi[:], raw_m1[u.parity][:, MG:MG + D]).then_inc(M["wg_hi"], 1)

            def split_second(u, user):
                if user:
                    v.wait_ge(M["u_done"] if user.kind == "m" else stages[user.kind]["k_done"], user.done())
                if u.kind == "a":
                    nc.vector.tensor_copy(wk_hi[:, 0:P], raw_a1[u.parity][:, AK:AK + P]).then_inc(A["wk_hi"], 1)
                elif u.kind == "b":
                    nc.vector.tensor_copy(wk_hi[:], raw_b1[u.parity][:, D:2 * D]).then_inc(B["wk_hi"], 1)
                else:
                    nc.vector.tensor_copy(wk_hi[:], raw_m1[u.parity][:, MU:MU + D]).then_inc(M["wu_hi"], 1)

            def split_values(u, user):
                if user.kind == "b":
                    v.wait_ge(B["v_done"], user.done())
                nc.vector.tensor_copy(wv_hi[:], raw_b1[u.parity][:, 2 * D:3 * D]).then_inc(B["wv_hi"], 1)

            def split_out(u):
                prev = u.prev()
                if u.kind == "b":
                    if prev.kind == "b":
                        v.wait_ge(B["wo_done"], prev.done())
                    v.wait_ge(ld_b2[u.parity], u.loads())
                    nc.vector.tensor_copy(wo_hi[:], raw_b2[u.parity][:]).then_inc(B["wo_hi"], 1)
                else:
                    v.wait_ge(M["down"] if prev.kind == "m" else B["wo_done"], prev.done())
                    v.wait_ge(ld_m2[u.parity], u.loads())
                    nc.vector.tensor_copy(wo_hi[:], raw_m2[u.parity][:]).then_inc(M["wd_hi"], 1)

            def hidden(u):
                if u.needs_tokens:
                    v.wait_ge(unit_w_ready, u.half + 1)
                if u.static and u.i >= CH - SHARED:
                    weights = ones[:].to_broadcast([P, HT])
                else:
                    weights = unit_w[u.half][:, u.offset % GROUPS, :]
                v.wait_ge(M["silu"], u.done())
                nc.vector.tensor_tensor(gu[:], gs[:], weights, ALU.mult).then_inc(M["weighted"], 1)
                v.wait_ge(M["weighted"], u.done())
                v.wait_ge(M["u_done"], u.done())
                if not u.very_first:
                    v.wait_ge(M["hh_hi"], u.done(1))
                nc.vector.tensor_tensor(hh[:], up_bank(u)[:], gu[:], ALU.mult).then_inc(M["hh"], 1)

            def split_hidden(u):
                v.wait_ge(M["hh_hi"], u.done())
                nc.vector.tensor_tensor(pv_lo[:], hh[:], pv_hi[:], ALU.subtract).then_inc(M["hh_lo"], 1)

            def read_acc(last):
                kind, half = last.kind, last.half
                v.wait_ge(stages[kind]["down" if kind == "m" else "wo_done"], last.done())
                for b in range(2):
                    two = slice(2 * b, 2 * b + 2)
                    part = acc[b][:].rearrange("p (t d) -> p t d", d=D)
                    if kind == "a":
                        add = nc.vector.scalar_tensor_tensor(xs[:, half, two], part, tg[:, 0:1], xs[:, half, two],
                                                             ALU.mult, ALU.add)
                    else:
                        add = nc.vector.tensor_tensor(ys[:, half, two], part, ys[:, half, two], ALU.add)
                add.then_inc(acc_free, 1)
                v.wait_ge(acc_free, STAGES.index((kind, half)) + 1)

            def finish(half):
                nc.vector.scalar_tensor_tensor(xs[:, half], ys[:, half], tg[:, 1:2], xs[:, half],
                                               ALU.mult, ALU.add).then_inc(out_ready, 1)

            def head(u):
                prev, nxt = u.prev(), u.next()
                after = nxt.next()
                softmax(u)
                take_q(nxt)
                split_first(after, nxt)
                if nxt.kind == "m":
                    hidden(nxt)
                split_second(after, nxt)
                if u.first and prev:
                    read_acc(prev)
                prepare_piece(*piece_at(u), u)
                if u.kind == "b":
                    split_out(u)
                if u.kind == "a" and u.half == 0:
                    v.wait_ge(A["vo_hi"], u.done())
                    this = bass.ds(u.i, 1)
                    nc.vector.tensor_tensor(vo_lo[:, this, :].squeeze(1), bank_v[:, 0:D], vo_hi[:, this, :].squeeze(1),
                                            ALU.subtract).then_inc(A["vo_lo"], 1)
                if after.kind == "b":
                    split_values(after, nxt)
                if nxt.kind == "b":
                    v.wait_ge(B["vtr_done"], nxt.done())
                    nc.vector.tensor_copy(vs[:], tiles(bank_t[:])).then_inc(B["vs"], 1)
                if not u.deferred:
                    split_pv(u)

            def chunk(u):
                nxt = u.next()
                after = nxt.next() if nxt else None
                if u.very_first:
                    read_acc(u.prev())
                    split_hidden(u)
                    split_out(u)
                if after:
                    split_first(after, nxt)
                if nxt:
                    hidden(nxt)
                if after:
                    split_second(after, nxt)
                prepare_piece(*piece_at(u), u)
                if u.last:
                    read_acc(u)
                if nxt:
                    split_hidden(nxt)
                    split_out(nxt)
                if u.last:
                    finish(u.half)

            prepare_piece("stats", ("x", 0))
            v.wait_ge(ld_small, 16)
            v.wait_ge(setup_pool, SETUP)
            nc.vector.scalar_tensor_tensor(gqk[:], sm[:, SM_GQ:SM_GQ + 1], SCALE, sm[:, SM_GK:SM_GK + 1],
                                           ALU.mult, ALU.mult).then_inc(setup_dve, 1)
            start = first_unit("a", 0)
            split_first(start, None)
            split_second(start, None)
            v.wait_ge(setup_act, 1)
            prepare_piece("norm", ("x", 0))
            prepare_piece("turn", ("x", 0))
            take_q(start)
            split_first(start.next(), start)
            split_second(start.next(), start)
            for kind, half in STAGES:
                run_units(v, kind, half, chunk if kind == "m" else head)

        @block.gpsimd
        def _(pool):
            def rest(lo, raw, hi, signal):
                nc.gpsimd.tensor_tensor(lo, raw, hi, ALU.subtract).then_inc(signal, 1)

            def split_first(u):
                if u.kind == "a":
                    pool.wait_ge(A["wq_hi"], u.done())
                    rest(wq_lo[:], raw_a1[u.parity][:, AQ:AQ + D], wq_hi[:], A["wq_lo"])
                elif u.kind == "b":
                    pool.wait_ge(B["wq_hi"], u.done())
                    rest(wq_lo[:], raw_b1[u.parity][:, 0:D], wq_hi[:], B["wq_lo"])
                else:
                    pool.wait_ge(M["wg_hi"], u.done())
                    rest(wq_lo[:], raw_m1[u.parity][:, MG:MG + D], wq_hi[:], M["wg_lo"])

            def split_second(u):
                if u.kind == "a":
                    pool.wait_ge(A["wk_hi"], u.done())
                    rest(wk_lo[:, 0:P], raw_a1[u.parity][:, AK:AK + P], wk_hi[:, 0:P], A["wk_lo"])
                elif u.kind == "b":
                    pool.wait_ge(B["wk_hi"], u.done())
                    rest(wk_lo[:], raw_b1[u.parity][:, D:2 * D], wk_hi[:], B["wk_lo"])
                else:
                    pool.wait_ge(M["wu_hi"], u.done())
                    rest(wk_lo[:], raw_m1[u.parity][:, MU:MU + D], wk_hi[:], M["wu_lo"])

            def split_values(u):
                pool.wait_ge(B["wv_hi"], u.done())
                rest(wv_lo[:], raw_b1[u.parity][:, 2 * D:3 * D], wv_hi[:], B["wv_lo"])

            def split_out(u):
                if u.kind == "b":
                    pool.wait_ge(B["wo_hi"], u.done())
                    rest(wo_lo[:], raw_b2[u.parity][:], wo_hi[:], B["wo_lo"])
                else:
                    pool.wait_ge(M["wd_hi"], u.done())
                    rest(wo_lo[:], raw_m2[u.parity][:], wo_hi[:], M["wd_lo"])

            def split_squares(u):
                if u.kind == "a":
                    pool.wait_ge(A["sq_k_hi"], u.done())
                    rest(sq_k_lo[:], sq_k[:], sq_k_hi[:], A["sq_k_lo"])

            def add_logs(u):
                pool.wait_ge(A["ln_k"], u.done())
                nc.gpsimd.tensor_tensor(ln_qk[:], ln_k[:], ln_q[:].unsqueeze(2).to_broadcast([P, NT, SEQ]), ALU.add)\
                    .then_inc(A["ln_qk"], 1)

            def head(u):
                nxt = u.next()
                after = nxt.next()
                split_squares(nxt)
                split_first(after)
                split_second(after)
                if u.kind == "b":
                    split_out(u)
                if after.kind == "b":
                    split_values(after)
                if nxt.kind == "a":
                    add_logs(nxt)
            
            def chunk(u):
                nxt = u.next()
                after = nxt.next() if nxt else None
                if u.very_first:
                    split_out(u)
                if after:
                    split_first(after)
                    split_second(after)
                if nxt:
                    split_out(nxt)

            nc.gpsimd.memset(zeros[:].bitcast(F32), 0.0).then_inc(setup_pool, 1)
            nc.gpsimd.memset(ones[:], 1.0).then_inc(setup_pool, 1)
            nc.gpsimd.memset(attn[:], 0.0).then_inc(setup_pool, 1)
            nc.gpsimd.memset(eps5[:], 1e-5).then_inc(setup_pool, 1)
            nc.gpsimd.memset(eps6[:], 1e-6).then_inc(setup_pool, 1)
            nc.gpsimd.memset(ones_of[:].bitcast(F32), 0.0).then_inc(setup_pool, 1)
            pool.wait_ge(setup_pool, SETUP - SPB)
            for s in range(SPB):
                nc.gpsimd.memset(ones_of[:, s, s * SEQ:(s + 1) * SEQ].bitcast(F32), 1.0).then_inc(setup_pool, 1)
            def split_context(half):
                pool.wait_ge(ctxt_hi_ready, half + 1)
                toks = slice(half * HT, (half + 1) * HT)
                rest(ctxt_lo[:, toks], ctxt[:, toks], ctxt_hi[:, toks], ctxt_lo_ready)

            start = first_unit("a", 0)
            split_first(start)
            split_second(start)
            split_context(0)
            split_squares(start)
            split_first(start.next())
            split_second(start.next())
            split_context(1)
            add_logs(start)
            for kind, half in STAGES:
                run_units(pool, kind, half, chunk if kind == "m" else head)


_INS = ["x", "ctx_t", "ctx", "head_a", "head_b", "chunk_m", "small"]


def lay_out(i, np):
    a = {k: np.asarray(v) for k, v in i.items()}
    f = np.float32
    x = a["x"].reshape(-1, a["x"].shape[-1])
    D = x.shape[1]
    ctx = a["ctx_1024"].reshape(x.shape[0], -1)
    C = ctx.shape[1]
    K = D // P

    def in_heads(w, chunks):
        h = w.shape[1] // P
        return w.reshape(chunks, P, h, P).transpose(2, 1, 0, 3).reshape(h, P, chunks * P)

    def out_heads(w):
        return w.reshape(-1, P, w.shape[1])

    wv_t = a["L0_xattn_Wv"].reshape(C, -1, P).transpose(1, 2, 0)
    head_a = np.concatenate([in_heads(a["L0_xattn_Wq"], K), in_heads(a["L0_xattn_Wk"], 1), wv_t,
                             out_heads(a["L0_xattn_Wo"])], axis=2)
    head_b = np.concatenate([in_heads(a["L0_ffn_wq"], K), in_heads(a["L0_ffn_wk"], K), in_heads(a["L0_ffn_wv"], K),
                             out_heads(a["L0_ffn_wo"])], axis=2)
    E, I, _ = a["L0_ffn_eg_w"].shape
    units = 2 * P // E

    def in_chunks(experts, shared):
        e = experts.reshape(2, E // 2, I // units, units, D).transpose(2, 0, 1, 3, 4).reshape(E * I, D)
        pad = np.zeros((-shared.shape[0] % P, D), f)
        return np.concatenate([e, shared, pad])

    gate = in_chunks(a["L0_ffn_eg_w"], a["L0_ffn_sg_w"])
    up = in_chunks(a["L0_ffn_eu_w"], a["L0_ffn_su_w"])
    down = in_chunks(a["L0_ffn_ed_w"].transpose(0, 2, 1), a["L0_ffn_sd_w"].T)
    chunk_m = np.concatenate([in_heads(gate.T, K), in_heads(up.T, K), down.reshape(-1, P, D)], axis=2)
    query, key = np.arange(P)[:, None] % SEQ, np.arange(SEQ)[None]
    mask = np.where(key <= query, f(0), f(-1e30)).astype(f)
    tie = np.tril(np.ones((E, E), f), -1).reshape(1, -1)
    small = np.concatenate([
        a["L0_xattn_gq"].reshape(P, 1), a["L0_xattn_gk"].reshape(P, 1),
        a["L0_ffn_ln1_w"].reshape(K, P).T, a["L0_ffn_ln2_w"].reshape(K, P).T,
        np.broadcast_to(a["g_xattn"].reshape(1, 1), (P, 1)), np.broadcast_to(a["g_ffn"].reshape(1, 1), (P, 1)),
        a["L0_ffn_gate_w"].T.reshape(K, P, E).transpose(1, 0, 2).reshape(P, K * E),
        np.eye(P, dtype=f), mask, np.broadcast_to(tie, (P, E * E))], axis=1)
    return {"x": x, "ctx_t": ctx.T, "ctx": ctx, "head_a": head_a, "head_b": head_b, "chunk_m": chunk_m, "small": small}


def kernel(**inputs):
    import concourse.bacc as bacc
    import numpy as np
    from concourse.bass_utils import run_bass_kernel_spmd

    laid = {k: np.ascontiguousarray(v) for k, v in lay_out(inputs, np).items()}
    nc = bacc.Bacc("TRN2", target_bir_lowering=False, num_devices=1)
    aps = [nc.dram_tensor(f"in_{n}", laid[n].shape, mybir.dt.from_np(laid[n].dtype), kind="ExternalInput").ap() for n in _INS]
    out = nc.dram_tensor("out", laid["x"].shape, F32, kind="ExternalOutput").ap()
    flamingo_layer(nc, *aps, out, inputs["L0_ffn_sg_w"].shape[0])
    r = run_bass_kernel_spmd(nc, [{f"in_{n}": laid[n] for n in _INS}], core_ids=[0])
    return r.results[0]["out"].reshape(inputs["x"].shape)
```

```python
from contextlib import ExitStack

import concourse.bass as bass
from concourse import mybir

F32 = mybir.dt.float32
F32R = mybir.dt.float32r
ALU = mybir.AluOpType
ACT = mybir.ActivationFunctionType
AX = mybir.AxisListType.X

P = 128
LN_EXP = "natural_log_exp_and_others"
SEQ = 64
HALVES = 2


class Counter:

    def __init__(self, sem):
        self.sem, self.n = sem, 0

    def mark(self, instruction):
        instruction.then_inc(self.sem, 1)
        self.n += 1

    def link(self, engine, instruction):
        self.mark(instruction)
        engine.wait_ge(self.sem, self.n)


class Unit:

    def __init__(self, plan, kind, half, offset, j=0):
        self.plan, self.kind, self.half, self.offset, self.j = plan, kind, half, offset, j
        self.count = plan.counts[kind]
        self.i = j * 2 + offset
        before = half * self.count + offset
        self.parity = before % 2
        self.odd = offset % 2 == 1
        self.pair = j + before // 2
        self.static = isinstance(j, int)
        self.first = self.static and self.i == 0
        self.last = self.static and self.i == self.count - 1
        self.very_first = self.first and half == 0
        self.deferred = kind == "a" and not (self.last and half == HALVES - 1)
        self.in_first_pair = self.static and self.i < 2 and half == 0
        self.stage_number = plan.stages.index((kind, half))
        self.needs_tokens, self.tokens_number = self.first, self.stage_number + 1

    def next(self):
        if not self.last:
            return Unit(self.plan, self.kind, self.half, self.offset + 1, self.j)
        if self.stage_number + 1 < len(self.plan.stages):
            return Unit(self.plan, *self.plan.stages[self.stage_number + 1], 0)
        return None

    def prev(self):
        if not self.first:
            return Unit(self.plan, self.kind, self.half, self.offset - 1, self.j)
        if self.stage_number:
            kind, half = self.plan.stages[self.stage_number - 1]
            return Unit(self.plan, kind, half, self.plan.counts[kind] - 1)
        return None

    def done(self, back=0):
        return self.j * 2 + (self.half * self.count + self.offset + 1 - back)

    def pair_number(self):
        return self.j + (self.half * (self.count // 2) + self.offset // 2 + 1)

    def loads(self):
        return self.pair * 16 + 16


class Plan:

    def __init__(self, stages, counts, straight, pieces):
        self.stages, self.counts, self.straight, self.pieces = stages, counts, straight, pieces

    def piece(self, u):
        return self.pieces.get((u.kind, u.half, u.i), (None, None)) if u.static else (None, None)

    def run(self, engine, kind, half, body):
        beside = [i for k, h, i in self.pieces if (k, h) == (kind, half)]
        looped = (min(beside + [self.straight[kind]]) - 1) // 2
        body(Unit(self, kind, half, 0))
        with engine.Fori(0, looped) as j:
            body(Unit(self, kind, half, 1, j))
            body(Unit(self, kind, half, 2, j))
        for i in range(1 + 2 * looped, self.counts[kind]):
            body(Unit(self, kind, half, i))


def plan_of(heads, chunks, shared_chunks):
    pieces = {}

    def beside(kind, half, start, names, step):
        for n, name in enumerate(names.split()):
            pieces[kind, half, start + n] = (name, step)

    beside("a", 0, heads - 4, "stats norm turn", ("x", 1))
    beside("a", 1, heads - 7, "stats norm sums root scale turn", ("y", 0))
    beside("b", 0, heads - 7, "stats norm sums root scale turn", ("y", 1))
    experts = "sums root scale turn logits equals ties better ranks best weights spread"
    beside("b", 1, heads - 13, experts, ("t", 0))
    beside("m", 0, chunks - 14, experts, ("t", 1))
    beside("m", 0, chunks - 2, "blend", ("t", 0))
    beside("m", 1, chunks - shared_chunks - 1, "blend", ("t", 1))
    stages = [(kind, half) for kind in "abm" for half in range(HALVES)]
    return Plan(stages, {"a": heads, "b": heads, "m": chunks},
                {"a": heads - 2, "b": heads - 2, "m": chunks - shared_chunks - 1}, pieces)


def flamingo_layer(nc, x, ctx_t, ctx, head_a, head_b, pair_v, chunk_m, small, out, shared_units):
    TOK, D = x.shape
    H = head_a.shape[0]
    C = ctx.shape[1]
    CH = chunk_m.shape[0]
    E = 16
    SETUP = 8
    TOP = 6
    WARM_UP = 20
    HT = TOK // HALVES
    NT = HT // P
    KD = D // P
    SPB = P // SEQ
    NS = HT // SEQ
    SCALE = float(P) ** -0.5
    UNITS = 2 * P // E
    GROUPS = 2
    SHARED = -(-shared_units // P)
    assert C == P and D == 2 * P and HT == 512
    AQ, AK, AV, AO = 0, D, 0, C
    A1, A2 = D + P, C + D
    B1, B2 = 2 * D, D
    PAIR = 2 * P
    MG, MU = 0, D
    M1, M2 = 2 * D, D
    SM_GQ, SM_GK, SM_LN1, SM_LN2, SM_GX, SM_GF, SM_GATE = 0, 1, 2, 4, 6, 7, 8
    SM_ID = SM_GATE + KD * E
    SM_MASK = SM_ID + P
    SM_TIE = SM_MASK + SEQ
    SM_W = SM_TIE + E * E

    with ExitStack() as stack:
        def sb(name, shape, dt=F32):
            return stack.enter_context(nc.sbuf_tensor(name, shape, dt))

        def psum(name):
            return stack.enter_context(nc.psum_tensor(name, [P, 512], F32))

        def sem(name):
            return stack.enter_context(nc.semaphore(name))

        sm = sb("sm", [P, SM_W])
        ident = sm[:, SM_ID:SM_ID + P]
        xs = sb("xs", [P, HALVES, NT, D])
        ys = sb("ys", [P, HALVES, NT, D])
        ctx_sb = sb("ctx_sb", [P, HALVES * NT, C])
        ctxt = sb("ctxt", [P, TOK])
        ctxt_hi, ctxt_lo = sb("ctxt_hi", [P, TOK], F32R), sb("ctxt_lo", [P, TOK], F32R)
        xt = sb("xt", [P, KD, HT])
        xt_hi = [sb(f"xt_hi{h}", [P, KD, HT], F32R) for h in range(HALVES)]
        xt_lo = [sb(f"xt_lo{h}", [P, KD, HT], F32R) for h in range(HALVES)]
        hn = sb("hn", [P, NT, D])
        ones, ones_of = sb("ones", [P, 1]), sb("ones_of", [P, SPB, P], F32R)
        zeros = sb("zeros", [P, 512], F32R)
        eps5, eps6 = sb("eps5", [P, 1]), sb("eps6", [P, 1])
        tg = sb("tg", [P, 2])
        gqk = sb("gqk", [P, 1])
        raw_a1 = [sb(f"raw_a1_{p}", [P, A1]) for p in range(2)]
        raw_a2 = [sb(f"raw_a2_{p}", [P, A2]) for p in range(2)]
        raw_b1 = [sb(f"raw_b1_{p}", [P, B1]) for p in range(2)]
        raw_b2 = [sb(f"raw_b2_{p}", [P, B2]) for p in range(2)]
        raw_m1 = [sb(f"raw_m1_{p}", [P, M1]) for p in range(2)]
        raw_m2 = [sb(f"raw_m2_{p}", [P, M2]) for p in range(2)]
        def halves_of(name, shape):
            return [[sb(f"{name}_{part}{p}", shape, F32R) for p in range(2)] for part in ("hi", "lo")]

        wq_hi, wq_lo = halves_of("wq", [P, D])
        wk_hi, wk_lo = halves_of("wk", [P, D])
        wo_hi, wo_lo = halves_of("wo", [P, D])
        raw_v = sb("raw_v", [P, KD * PAIR])
        wv_hi, wv_lo = sb("wv_hi", [P, KD * PAIR], F32R), sb("wv_lo", [P, KD * PAIR], F32R)
        vo_hi, vo_lo = sb("vo_hi", [P, H, D], F32R), sb("vo_lo", [P, H, D], F32R)
        sq_q, sq_k = sb("sq_q", [P, HT]), sb("sq_k", [P, HT])
        sq_k_hi, sq_k_lo = sb("sq_k_hi", [P, HT], F32R), sb("sq_k_lo", [P, HT], F32R)
        qt, kt = sb("qt", [P, HT]), sb("kt", [P, HT])
        vs = sb("vs", [P, NT, PAIR])
        ln_k, ln_q = sb("ln_k", [P, NT, SEQ]), sb("ln_q", [P, NT])
        ln_qk, r_qk = sb("ln_qk", [P, NT, SEQ]), sb("r_qk", [P, NT, SEQ])
        sc = sb("sc", [P, NT, SEQ])
        sc_max = sb("sc_max", [P, NT])
        sc_sub = sb("sc_sub", [P, NT, SEQ])
        ex = sb("ex", [P, NT, SEQ])
        ex_sum, ex_inv = sb("ex_sum", [P, NT]), sb("ex_inv", [P, NT])
        attn = sb("attn", [P, NT, P])
        attn_t = sb("attn_t", [P, HT])
        pv_hi, pv_lo = halves_of("pv", [P, HT])
        gs, gu, hh = sb("gs", [P, HT]), sb("gu", [P, HT]), sb("hh", [P, HT])
        unit_w = [sb(f"unit_w{h}", [P, GROUPS, HT]) for h in range(HALVES)]
        bn = sb("bn", [P, NT, 6])
        mv = sb("mv", [P, NT, 2])
        ms = sb("ms", [P, NT])
        st = sb("st", [P, 8, NT])
        junk = sb("junk", [P, D])
        rt = sb("rt", [P, 6, NT, E])
        rmax = sb("rmax", [P, 4, NT])
        pair1, pair2 = sb("pair1", [P, NT, E, E]), sb("pair2", [P, NT, E, E])
        cw = sb("cw", [P, NT, E, UNITS])

        acc = [psum("acc0"), psum("acc1")]
        bank_q, bank_k, bank_v = psum("bank_q"), psum("bank_k"), psum("bank_v")
        bank_s, bank_t, bank_p = psum("bank_s"), psum("bank_t"), psum("bank_p")

        ld_small, ld_ctx = sem("ld_small"), sem("ld_ctx")
        ld_ctxt = [sem(f"ld_ctxt{h}") for h in range(HALVES)]
        ld_x = [[sem(f"ld_x{h}_{t}") for t in range(NT)] for h in range(HALVES)]
        ld_a1 = [sem(f"ld_a1_{p}") for p in range(2)]
        ld_a2 = [sem(f"ld_a2_{p}") for p in range(2)]
        ld_b1 = [sem(f"ld_b1_{p}") for p in range(2)]
        ld_b2 = [sem(f"ld_b2_{p}") for p in range(2)]
        ld_v = sem("ld_v")
        ld_m1 = [sem(f"ld_m1_{p}") for p in range(2)]
        ld_m2 = [sem(f"ld_m2_{p}") for p in range(2)]
        st_out = sem("st_out")

        def stage_sems(tag, names):
            return {n: sem(f"{tag}_{n}") for n in names.split()}

        A = stage_sems("a", "wq_hi wq_lo wk_hi wk_lo q_done k_done sq_q sq_k sq_k_hi sq_k_lo qt kt scores scaled max "
                       "sub exp sum inv norm_lo norm_hi t_done attn_t vo_done vo_hi vo_lo ssk_done ssq_done ln_q "
                       "ln_k ln_qk r_qk pv_done pv_hi pv_lo wo_done")
        B = stage_sems("b", "wq_hi wq_lo wk_hi wk_lo wv_hi wv_lo wo_hi wo_lo q_done k_done v_done qt kt vs scores "
                       "scaled max sub exp sum inv norm_lo norm_hi t_done attn_t pv_done pv_hi pv_lo wo_done")
        M = stage_sems("m", "wg_hi wg_lo wu_hi wu_lo wd_hi wd_lo g_done u_done silu weighted hh hh_hi hh_lo down")

        dve, act = Counter(sem("dve_step")), Counter(sem("act_step"))
        pe_tr = sem("pe_tr")
        pe_gate = sem("pe_gate")
        pe_cw = sem("pe_cw")
        tok_ready = sem("tok_ready")
        cw_ready = sem("cw_ready")
        var_ready, rough = sem("var_ready"), sem("rough")
        y_ready = sem("y_ready")
        xt_ready, xt_hi_ready, xt_lo_ready = sem("xt_ready"), sem("xt_hi_ready"), sem("xt_lo_ready")
        logits_sub, logits_exp = sem("logits_sub"), sem("logits_exp")
        unit_w_ready = sem("unit_w_ready")
        acc_free = sem("acc_free")
        setup_pool, setup_dve, setup_act = sem("setup_pool"), sem("setup_dve"), sem("setup_act")
        ctxt_hi_ready, ctxt_lo_ready = sem("ctxt_hi_ready"), sem("ctxt_lo_ready")
        down_part = sem("down_part")
        out_ready = sem("out_ready")

        def tiles(ap):
            return ap.rearrange("p (t n) -> p t n", t=NT)

        stages = {"a": A, "b": B, "m": M}
        plan = plan_of(H, CH, SHARED)
        STAGES = plan.stages
        PREP = {(step, half): n for n, (step, half) in enumerate((s_, h_) for s_ in "xyt" for h_ in range(HALVES))}
        piece_at, run_units = plan.piece, plan.run

        def first_unit(kind, half):
            return Unit(plan, kind, half, 0)

        def turn_banks(u):
            return (bank_p, {"a": bank_v, "b": bank_s, "m": bank_t}[u.kind])

        def gate_bank(u):
            return (bank_q, bank_v)[u.parity]

        def up_bank(u):
            return (bank_k, bank_s)[u.parity]

        block = stack.enter_context(nc.Block())

        @block.sync
        def _(sp):
            x_v = x.rearrange("(h t p) d -> h p t d", h=HALVES, p=P)
            out_v = out.rearrange("(h t p) d -> h p t d", h=HALVES, p=P)

            def load(buffers, landed, weights, cols, u):
                sp.dma_start(buffers[u.parity][:], weights[bass.ds(u.i, 1), :, cols].rearrange("h p n -> p (h n)"))\
                    .then_inc(landed[u.parity], 16)

            def load_a1(u):
                load(raw_a1, ld_a1, head_a, slice(0, A1), u)

            def load_a2(u):
                load(raw_a2, ld_a2, head_a, slice(A1, A1 + A2), u)

            def load_b1(u):
                load(raw_b1, ld_b1, head_b, slice(0, B1), u)

            def load_b2(u):
                load(raw_b2, ld_b2, head_b, slice(B1, B1 + B2), u)

            def load_v(first):
                pair = first.j + first.offset // 2
                sp.dma_start(raw_v[:], pair_v[bass.ds(pair, 1)].rearrange("h p n -> p (h n)")).then_inc(ld_v, 16)

            def load_m1(u):
                load(raw_m1, ld_m1, chunk_m, slice(0, M1), u)

            def load_m2(u):
                load(raw_m2, ld_m2, chunk_m, slice(M1, M1 + M2), u)

            def load_x(half):
                for t in range(NT):
                    sp.dma_start(xs[:, half, t], x_v[half, :, t]).then_inc(ld_x[half][t], 16)

            load_x(0)
            sp.dma_start(sm[:], small).then_inc(ld_small, 16)
            load_a1(first_unit("a", 0))
            sp.dma_start(ctxt[:, 0:HT], ctx_t[:, 0:HT]).then_inc(ld_ctxt[0], 16)
            load_a1(first_unit("a", 0).next())
            load_a2(first_unit("a", 0))
            sp.dma_start(ctx_sb[:], ctx.rearrange("(t p) c -> p t c", p=P)).then_inc(ld_ctx, 16)
            load_a2(first_unit("a", 0).next())
            sp.dma_start(ctxt[:, HT:TOK], ctx_t[:, HT:TOK]).then_inc(ld_ctxt[1], 16)
            load_x(1)
            load_v(first_unit("b", 0))
            for i in range(2):
                load_b1(Unit(plan, "b", 0, i))
                load_b2(Unit(plan, "b", 0, i))
                load_m1(Unit(plan, "m", 0, i))
                load_m2(Unit(plan, "m", 0, i))

            def refill(kind, half, loads):
                def unit(u):
                    if kind == "b" and not u.odd:
                        sp.wait_ge(B["wv_lo"], u.pair_number() - 1)
                        load_v(u)
                    for load, users in loads:
                        for user in users:
                            sp.wait_ge(user, u.done(2))
                        load(u)
                count = plan.counts[kind]
                start = 0 if half else 2
                pairs = (count - start) // 2
                with sp.Fori(0, pairs) as j:
                    unit(Unit(plan, kind, half, start, j))
                    unit(Unit(plan, kind, half, start + 1, j))
                if (count - start) % 2:
                    unit(Unit(plan, kind, half, count - 1))

            refill("a", 0, [(load_a1, (A["wq_lo"], A["wk_lo"])), (load_a2, (A["vo_done"],))])
            refill("a", 1, [(load_a1, (A["wq_lo"], A["wk_lo"]))])
            for half in range(HALVES):
                refill("b", half, [(load_b1, (B["wq_lo"], B["wk_lo"])), (load_b2, (B["wo_lo"],))])
            for half in range(HALVES):
                refill("m", half, [(load_m1, (M["wg_lo"], M["wu_lo"])), (load_m2, (M["wd_lo"],))])
            for half in range(HALVES):
                for b in range(2):
                    sp.wait_ge(out_ready, 2 * half + b + 1)
                    sp.dma_start(out_v[half, :, 2 * b:2 * b + 2], xs[:, half, 2 * b:2 * b + 2]).then_inc(st_out, 16)
            sp.wait_ge(st_out, 16 * 2 * HALVES)

        @block.tensor
        def _(pe):
            def project(bank, w_hi, w_lo, m_hi, m_lo, chunks=KD):
                n = 0
                for k in range(chunks):
                    cols = slice(k * P, (k + 1) * P)
                    for w, m in ((w_hi, m_hi), (w_hi, m_lo), (w_lo, m_hi)):
                        last = nc.tensor.matmul(bank[:], w[:, cols], m(k), start=n == 0, stop=n == 3 * chunks - 1)
                        n += 1
                return last

            def tokens_hi(u):
                return lambda k: xt_hi[u.half][:, k, :]

            def tokens_lo(u):
                return lambda k: xt_lo[u.half][:, k, :]

            def clear_acc(u):
                if u.stage_number:
                    if u.kind == "m" and u.half:
                        pe.wait_ge(out_ready, 2)
                    else:
                        pe.wait_ge(acc_free, 2 * u.stage_number)
                for bank in acc:
                    last = nc.tensor.matmul(bank[:], zeros[:, 0:P], zeros[:], start=True, stop=True, skip_group_check=True)

            def output(u):
                if u.kind == "a":
                    pe.wait_ge(A["pv_lo"], u.done())
                    if u.half == 0:
                        pe.wait_ge(A["vo_lo"], u.done())
                    w_hi, w_lo = vo_hi[:, bass.ds(u.i, 1), :].squeeze(1), vo_lo[:, bass.ds(u.i, 1), :].squeeze(1)
                    done = A["wo_done"]
                elif u.kind == "b":
                    pe.wait_ge(B["pv_lo"], u.done())
                    pe.wait_ge(B["wo_lo"], u.done())
                    w_hi, w_lo = wo_hi[u.parity][:], wo_lo[u.parity][:]
                    done = B["wo_done"]
                else:
                    pe.wait_ge(M["hh_lo"], u.done())
                    pe.wait_ge(M["wd_lo"], u.done())
                    w_hi, w_lo = wo_hi[u.parity][:], wo_lo[u.parity][:]
                    done = M["down"]
                hi, lo = pv_hi[u.parity], pv_lo[u.parity]
                for t in range(NT):
                    tok = slice(t * P, (t + 1) * P)
                    for w, m in ((hi, w_hi), (hi, w_lo), (lo, w_hi)):
                        last = nc.tensor.matmul(acc[t // 2][:, (t % 2) * D:(t % 2 + 1) * D], w[:, tok], m,
                                                start=False, stop=True, skip_group_check=True)
                    if u.kind == "m" and u.last and t == 1:
                        last.then_inc(down_part, 1)
                last.then_inc(done, 1)

            def project_gate(u):
                if not u.in_first_pair:
                    pe.wait_ge(M["silu"], u.done(2))
                pe.wait_ge(M["wg_lo"], u.done())
                project(gate_bank(u), wq_hi[u.parity], wq_lo[u.parity], tokens_hi(u), tokens_lo(u)).then_inc(M["g_done"], 1)

            def project_up(u):
                if not u.in_first_pair:
                    pe.wait_ge(M["hh"], u.done(2))
                pe.wait_ge(M["wu_lo"], u.done())
                project(up_bank(u), wk_hi[u.parity], wk_lo[u.parity], tokens_hi(u), tokens_lo(u)).then_inc(M["u_done"], 1)

            def project_first(u):
                if u.needs_tokens:
                    pe.wait_ge(xt_lo_ready, u.tokens_number)
                if u.kind == "a":
                    pe.wait_ge(A["wq_lo"], u.done())
                    project(bank_q, wq_hi[u.parity], wq_lo[u.parity], tokens_hi(u), tokens_lo(u)).then_inc(A["q_done"], 1)
                elif u.kind == "b":
                    pe.wait_ge(B["wq_lo"], u.done())
                    project(bank_q, wq_hi[u.parity], wq_lo[u.parity], tokens_hi(u), tokens_lo(u)).then_inc(B["q_done"], 1)
                else:
                    project_gate(u)
                    project_up(u)

            def project_keys(u):
                if u.kind == "a":
                    pe.wait_ge(A["wk_lo"], u.done())
                    if u.needs_tokens:
                        pe.wait_ge(ctxt_lo_ready, u.half + 1)
                    toks = slice(u.half * HT, (u.half + 1) * HT)
                    project(bank_k, wk_hi[u.parity], wk_lo[u.parity], lambda k: ctxt_hi[:, toks], lambda k: ctxt_lo[:, toks], 1)\
                        .then_inc(A["k_done"], 1)
                elif u.kind == "b":
                    pe.wait_ge(B["wk_lo"], u.done())
                    project(bank_k, wk_hi[u.parity], wk_lo[u.parity], tokens_hi(u), tokens_lo(u)).then_inc(B["k_done"], 1)

            def project_values(first, second_tiles):
                number = first.pair_number()
                pe.wait_ge(B["wv_lo"], number)
                if second_tiles:
                    pe.wait_ge(B["vs"], number * 2 - 1)
                for b in range(NT // 2):
                    t = b + second_tiles * (NT // 2)
                    n = 0
                    for k in range(KD):
                        x_hi, x_lo = (x[first.half][:, k, t * P:(t + 1) * P] for x in (xt_hi, xt_lo))
                        cols = slice(k * PAIR, (k + 1) * PAIR)
                        for m, w in ((x_hi, wv_hi), (x_hi, wv_lo), (x_lo, wv_hi)):
                            last = nc.tensor.matmul(bank_v[:, b * PAIR:(b + 1) * PAIR], m, w[:, cols],
                                                    start=n == 0, stop=n == 3 * KD - 1)
                            n += 1
                last.then_inc(B["v_done"], 1)

            def value_out(u):
                pe.wait_ge(ld_a2[u.parity], u.loads())
                nc.tensor.matmul(bank_v[:, 0:D], raw_a2[u.parity][:, AV:AV + C], raw_a2[u.parity][:, AO:AO + D],
                                 start=True, stop=True).then_inc(A["vo_done"], 1)

            def norm_q(u):
                pe.wait_ge(A["sq_q"], u.done())
                for t in range(NT):
                    last = nc.tensor.matmul(bank_v[:, D + t:D + t + 1], sq_q[:, t * P:(t + 1) * P], ones[:],
                                            start=True, stop=True)
                last.then_inc(A["ssq_done"], 1)

            def norm_k(u):
                pe.wait_ge(A["sq_k_lo"], u.done())
                if not u.very_first:
                    pe.wait_ge(A["scaled"], u.done(1))
                for s in range(SPB):
                    for part, square in enumerate((sq_k_hi, sq_k_lo)):
                        keys = square[:].rearrange("p (t s k) -> p t s k", s=SPB, k=SEQ)[:, :, s, :]
                        first, final = s + part == 0, s + part == SPB
                        last = nc.tensor.matmul(bank_s[:, NT * SEQ:2 * NT * SEQ], ones_of[:, s, :], keys,
                                                start=first, stop=final)
                last.then_inc(A["ssk_done"], 1)

            def scores(u):
                stage = stages[u.kind]
                pe.wait_ge(stage["qt"], u.done())
                pe.wait_ge(stage["kt"], u.done())
                if u.kind == "a":
                    pe.wait_ge(A["ln_k"], u.done())
                for b in range(NS):
                    tok = slice(b * SEQ, (b + 1) * SEQ)
                    t, s = b // SPB, b % SPB
                    last = nc.tensor.matmul(bank_s[s * SEQ:(s + 1) * SEQ, t * SEQ:(t + 1) * SEQ], qt[:, tok], kt[:, tok],
                                            start=True, stop=True)
                last.then_inc(stage["scores"], 1)

            def turn_attn(u):
                stage = stages[u.kind]
                pe.wait_ge(stage["norm_hi"], u.done())
                for t in range(NT):
                    last = nc.tensor.transpose(bank_t[:, t * P:(t + 1) * P], attn[:, t, :], ident)
                last.then_inc(stage["t_done"], 1)

            def attn_values(u):
                stage = stages[u.kind]
                if u.kind == "a" and u.very_first:
                    pe.wait_ge(ld_ctx, 16)
                pe.wait_ge(stage["attn_t"], u.done())
                if u.kind == "b" and not u.odd:
                    pe.wait_ge(B["vs"], u.pair_number() * 2)
                for t in range(NT):
                    value = ctx_sb[:, u.half * NT + t, :] if u.kind == "a" else vs[:, t, u.odd * P:(u.odd + 1) * P]
                    last = nc.tensor.matmul(bank_p[:, t * P:(t + 1) * P], value, attn_t[:, t * P:(t + 1) * P],
                                            start=True, stop=True)
                last.then_inc(stage["pv_done"], 1)

            def turn_tokens(step, banks):
                pe.wait_ge(tok_ready, PREP[step] + 1)
                for k, bank in enumerate(banks):
                    for t in range(NT):
                        last = nc.tensor.transpose(bank[:, t * P:(t + 1) * P], hn[:, t, k * P:(k + 1) * P], ident)
                last.then_inc(pe_tr, 1)

            def prepare(u):
                piece, step = piece_at(u)
                if piece in ("turn", "spread") and u.kind == "b":
                    pe.wait_ge(B["scaled"], u.done())
                if piece == "turn":
                    turn_tokens(step, turn_banks(u))
                    return [(xt_lo_ready, PREP[step] + 1)]
                if piece == "logits":
                    pe.wait_ge(xt_ready, step[1] + 1)
                    pe.wait_ge(xt_lo_ready, PREP[step] + 1)
                    for t in range(NT):
                        for k in range(KD):
                            last = nc.tensor.matmul(bank_p[:, t * E:(t + 1) * E], xt[:, k, t * P:(t + 1) * P],
                                                    sm[:, SM_GATE + k * E:SM_GATE + (k + 1) * E],
                                                    start=k == 0, stop=k == KD - 1)
                    last.then_inc(pe_gate, 1)
                    return [(logits_sub, step[1] + 1)]
                if piece == "spread":
                    pe.wait_ge(cw_ready, step[1] + 1)
                    for g, bank in enumerate(turn_banks(u)):
                        experts = slice(g * E // GROUPS, (g + 1) * E // GROUPS)
                        for t in range(NT):
                            last = nc.tensor.transpose(bank[:, t * P:(t + 1) * P],
                                                       cw[:, t, experts, :].rearrange("p e n -> p (e n)"), ident)
                    last.then_inc(pe_cw, 1)
                    return [(unit_w_ready, step[1] + 1)]
                return []

            def head(u):
                prev, nxt = u.prev(), u.next()

                scores(u)
                if prev and prev.deferred:
                    attn_values(prev)
                if nxt.kind == "a":
                    project_keys(nxt)
                project_first(nxt)
                second_tiles = u.kind == "b" and not u.odd
                if second_tiles:
                    project_values(u, True)
                if u.kind == "a":
                    pe.wait_ge(A["ln_q"], u.done())
                if prev:
                    pe.wait_ge(stages[prev.kind]["pv_lo"], prev.done())
                held = prepare(u)
                if prev:
                    output(prev)
                if nxt.kind == "b" and not second_tiles:
                    project_keys(nxt)
                values_of_a = u.kind == "a" and u.half == 0
                if values_of_a and not held:
                    value_out(u)
                if nxt.kind == "a":
                    norm_k(nxt)
                turn_attn(u)
                if nxt.kind == "b" and second_tiles:
                    project_keys(nxt)
                for semaphore, value in held:
                    pe.wait_ge(semaphore, value)
                if values_of_a and held:
                    value_out(u)
                if nxt.kind == "a":
                    norm_q(nxt)
                if nxt.kind == "b" and not second_tiles:
                    project_values(nxt, False)
                if not u.deferred:
                    attn_values(u)
                if u.first:
                    clear_acc(u)

            def chunk(u):
                prev, nxt = u.prev(), u.next()
                if u.very_first:
                    project_gate(nxt)
                    output(prev)
                    project_up(nxt)
                elif nxt:
                    project_first(nxt)
                prepare(u)
                if u.first:
                    clear_acc(u)
                output(u)

            pe.wait_ge(setup_pool, SETUP)
            for _ in range(WARM_UP):
                nc.tensor.matmul(bank_s[:], zeros[:, 0:P], zeros[:], start=True, stop=True)
            pe.wait_ge(ld_small, 16)
            start = first_unit("a", 0)
            project_keys(start)
            turn_tokens(("x", 0), (bank_p, bank_t))
            for _ in range(WARM_UP // 2):
                nc.tensor.matmul(bank_s[:], zeros[:, 0:P], zeros[:], start=True, stop=True)
            project_first(start)
            norm_q(start)
            norm_k(start)
            for kind, half in STAGES:
                run_units(pe, kind, half, chunk if kind == "m" else head)

        @block.scalar
        def _(act_e):
            def rough_root(step):
                act_e.wait_ge(var_ready, PREP[step] + 1)
                act.link(act_e, nc.scalar.activation(st[:, 1, :], st[:, 0, :], ACT.Ln))
                nc.scalar.activation(st[:, 1, :], st[:, 1, :], ACT.Exp, scale=-0.5).then_inc(rough, 1)

            def mean_squares(source):
                for t in range(NT):
                    act.link(act_e, nc.scalar.activation(junk[:], source[:, t, :], ACT.Square, scale=float(D) ** -0.5,
                                                         accum_out=ms[:, t:t + 1]))

            def root_of_squares():
                act.link(act_e, nc.scalar.activation(st[:, 1, :], ms[:], ACT.Ln, bias=eps6[:, 0:1]))
                nc.scalar.activation(st[:, 1, :], st[:, 1, :], ACT.Exp, scale=-0.5).then_inc(rough, 1)

            def take_tokens(step, banks):
                kind, half = step
                act_e.wait_ge(pe_tr, PREP[step] + 1)
                if kind == "t" and half:
                    act_e.wait_ge(pe_gate, half)
                for k, bank in enumerate(banks):
                    def take(target):
                        if kind == "x":
                            return nc.scalar.activation(target[:, k, :], bank[:], ACT.Copy)
                        col = (SM_LN1 if kind == "y" else SM_LN2) + k
                        return nc.scalar.activation(target[:, k, :], bank[:], ACT.Identity, scale=sm[:, col:col + 1])
                    if kind == "t":
                        last = take(xt)
                    take(xt_hi[half]).then_inc(xt_hi_ready, 1)
                if kind == "t":
                    last.then_inc(xt_ready, 1)

            def prepare(u):
                piece, step = piece_at(u)
                if piece == "norm":
                    rough_root(step)
                if piece == "root":
                    if u.kind == "m":
                        act_e.preload_act_table_set(LN_EXP)
                    root_of_squares()
                if piece == "sums":
                    if step[0] == "y":
                        act_e.wait_ge(y_ready, step[1] + 1)
                    else:
                        act_e.wait_ge(acc_free, STAGES.index(("b", step[1])) * 2 + 2)
                    mean_squares(ys[:, step[1]])
                if piece == "turn":
                    take_tokens(step, turn_banks(u))
                if piece == "logits":
                    act_e.wait_ge(logits_sub, step[1] + 1)
                    nc.scalar.activation(rt[:, 1], rt[:, 0], ACT.Exp).then_inc(logits_exp, 1)
                if piece == "spread":
                    act_e.wait_ge(pe_cw, step[1] + 1)
                    for g, bank in enumerate(turn_banks(u)):
                        last = nc.scalar.activation(unit_w[step[1]][:, g, :], bank[:], ACT.Copy)
                    last.then_inc(unit_w_ready, 1)

            def square_q(u):
                act_e.wait_ge(A["q_done"], u.done())
                nc.scalar.activation(sq_q[:], bank_q[:], ACT.Square, scale=SCALE).then_inc(A["sq_q"], 1)

            def square_k(u):
                act_e.wait_ge(A["k_done"], u.done())
                nc.scalar.activation(sq_k[:], bank_k[:], ACT.Square, scale=SCALE).then_inc(A["sq_k"], 1)
                nc.scalar.activation(sq_k_hi[:], bank_k[:], ACT.Square, scale=SCALE).then_inc(A["sq_k_hi"], 1)

            def take_k(u):
                if u.kind == "a":
                    nc.scalar.activation(kt[:], bank_k[:], ACT.Identity, scale=gqk[:, 0:1]).then_inc(A["kt"], 1)
                if u.kind == "b":
                    act_e.wait_ge(B["k_done"], u.done())
                    nc.scalar.activation(kt[:], bank_k[:], ACT.Copy).then_inc(B["kt"], 1)

            def take_v(first, second_tiles):
                act_e.wait_ge(B["v_done"], first.pair_number() * 2 - (not second_tiles))
                at = second_tiles * (NT // 2)
                nc.scalar.activation(vs[:, at:at + NT // 2, :], bank_v[:].rearrange("p (t n) -> p t n", n=PAIR),
                                     ACT.Copy).then_inc(B["vs"], 1)

            def log_q(u):
                act_e.wait_ge(A["ssq_done"], u.done())
                nc.scalar.activation(ln_q[:], bank_v[:, D:D + NT], ACT.Ln, bias=eps5[:, 0:1]).then_inc(A["ln_q"], 1)

            def log_k(u):
                act_e.wait_ge(A["ssk_done"], u.done())
                nc.scalar.activation(ln_k[:], tiles(bank_s[:, NT * SEQ:2 * NT * SEQ]), ACT.Ln, bias=eps5[:, 0:1])\
                    .then_inc(A["ln_k"], 1)

            def roots(u):
                act_e.wait_ge(A["ln_qk"], u.done())
                nc.scalar.activation(r_qk[:], ln_qk[:], ACT.Exp, scale=-0.5).then_inc(A["r_qk"], 1)

            def take_values(u):
                stage = stages[u.kind]
                act_e.wait_ge(stage["pv_done"], u.done())
                nc.scalar.activation(pv_hi[u.parity][:], bank_p[:], ACT.Copy).then_inc(stage["pv_hi"], 1)

            def gate(u):
                act_e.wait_ge(M["g_done"], u.done())
                if not u.very_first:
                    act_e.wait_ge(M["weighted"], u.done(1))
                nc.scalar.activation(gs[:], gate_bank(u)[:], ACT.Silu).then_inc(M["silu"], 1)

            def split_hidden(u):
                act_e.wait_ge(M["hh"], u.done())
                if not u.in_first_pair:
                    act_e.wait_ge(M["down"], u.done(2))
                nc.scalar.activation(pv_hi[u.parity][:], hh[:], ACT.Copy).then_inc(M["hh_hi"], 1)

            def head(u):
                stage, nxt = stages[u.kind], u.next()
                if u.prev() and u.prev().deferred:
                    take_values(u.prev())
                if nxt.kind == "a":
                    square_k(nxt)
                act_e.wait_ge(stage["sub"], u.done())
                nc.scalar.activation(ex[:], sc_sub[:], ACT.Exp).then_inc(stage["exp"], 1)
                if nxt.kind == "a":
                    square_q(nxt)
                if nxt.kind == "m":
                    gate(nxt)
                if nxt.kind == "m" or nxt.next().kind == "m":
                    split_up(nxt.next(), u)
                second_tiles = u.kind == "b" and not u.odd
                if second_tiles:
                    take_v(u, True)
                prepare(u)
                if not second_tiles:
                    take_k(nxt)
                if nxt.kind == "a":
                    log_k(nxt)
                act_e.wait_ge(stage["t_done"], u.done())
                nc.scalar.activation(attn_t[:], bank_t[:], ACT.Copy).then_inc(stage["attn_t"], 1)
                if second_tiles:
                    take_k(nxt)
                if nxt.kind == "a":
                    log_q(nxt)
                if u.kind == "a" and u.half == 0:
                    act_e.wait_ge(A["vo_done"], u.done())
                    nc.scalar.activation(vo_hi[:, bass.ds(u.i, 1), :].squeeze(1), bank_v[:, 0:D], ACT.Copy)\
                        .then_inc(A["vo_hi"], 1)
                if not u.deferred:
                    take_values(u)
                if nxt.kind == "b" and not second_tiles:
                    take_v(nxt, False)
                if nxt.kind == "a":
                    roots(nxt)

            def split_down(u):
                if u.in_first_pair:
                    act_e.wait_ge(B["wo_done"], Unit(plan, "b", HALVES - 1, H - 2 + u.i).done())
                else:
                    act_e.wait_ge(M["down"], u.done(2))
                act_e.wait_ge(ld_m2[u.parity], u.loads())
                nc.scalar.activation(wo_hi[u.parity][:], raw_m2[u.parity][:], ACT.Copy).then_inc(M["wd_hi"], 1)

            def split_up(u, user):
                act_e.wait_ge(M["u_done"] if user.kind == "m" else B["k_done"], user.done())
                act_e.wait_ge(ld_m1[u.parity], u.loads())
                nc.scalar.activation(wk_hi[u.parity][:], raw_m1[u.parity][:, MU:MU + D], ACT.Copy).then_inc(M["wu_hi"], 1)

            def chunk(u):
                nxt = u.next()
                after = nxt.next() if nxt else None
                if u.very_first:
                    split_hidden(u)
                    split_down(u)
                if nxt:
                    gate(nxt)
                    split_down(nxt)
                if after:
                    split_up(after, u)
                if nxt:
                    split_hidden(nxt)
                prepare(u)

            def split_context(half):
                act_e.wait_ge(ld_ctxt[half], 16)
                toks = slice(half * HT, (half + 1) * HT)
                nc.scalar.activation(ctxt_hi[:, toks], ctxt[:, toks], ACT.Copy).then_inc(ctxt_hi_ready, 1)

            act_e.wait_ge(ld_small, 16)
            nc.scalar.activation(tg[:], sm[:, SM_GX:SM_GF + 1], ACT.Tanh).then_inc(setup_act, 1)
            act_e.preload_act_table_set(LN_EXP)
            split_context(0)
            act_e.wait_ge(setup_dve, 1)
            act_e.wait_ge(setup_pool, SETUP)
            rough_root(("x", 0))
            start = first_unit("a", 0)
            square_k(start)
            take_k(start)
            take_tokens(("x", 0), (bank_p, bank_t))
            square_q(start)
            log_q(start)
            log_k(start)
            roots(start)
            split_context(1)
            for kind, half in STAGES:
                run_units(act_e, kind, half, chunk if kind == "m" else head)

        @block.vector
        def _(v):
            def link(ins):
                dve.link(v, ins)

            roots_taken = Counter(rough)

            def await_root():
                roots_taken.n += 1
                v.wait_ge(rough, roots_taken.n)

            def refined_root():
                link(nc.vector.tensor_tensor(st[:, 3, :], st[:, 0, :], st[:, 1, :], ALU.mult))
                link(nc.vector.tensor_tensor(st[:, 4, :], st[:, 3, :], st[:, 1, :], ALU.mult))
                link(nc.vector.tensor_scalar(st[:, 5, :], st[:, 4, :], -0.5, 1.5, ALU.mult, ALU.add))
                link(nc.vector.tensor_tensor(st[:, 2, :], st[:, 1, :], st[:, 5, :], ALU.mult))

            def per_expert(ap):
                return ap.unsqueeze(2).to_broadcast([P, NT, E])

            mine = rt[:, 2].unsqueeze(3).to_broadcast([P, NT, E, E])
            others = rt[:, 2].unsqueeze(2).to_broadcast([P, NT, E, E])

            def prepare_piece(piece, step, u=None):
                if not piece:
                    return
                kind, half = step
                if piece == "stats":
                    for t in range(NT):
                        if kind == "x":
                            v.wait_ge(ld_x[half][t], 16)
                        dve.mark(nc.vector.bn_stats(bn[:, t, :], xs[:, half, t, :]))
                    v.wait_ge(dve.sem, dve.n)
                    for t in range(NT):
                        dve.mark(nc.vector.bn_aggr(mv[:, t, :], bn[:, t, :]))
                    v.wait_ge(dve.sem, dve.n)
                    nc.vector.tensor_scalar(st[:, 0, :], mv[:, :, 1], 1e-5, None, ALU.add).then_inc(var_ready, 1)
                if piece == "norm":
                    await_root()
                    refined_root()
                    target, signal = (hn[:], tok_ready) if kind == "x" else (ys[:, half], y_ready)
                    if kind == "x" and PREP[step]:
                        v.wait_ge(pe_tr, PREP[step])
                    for t in range(NT):
                        last = nc.vector.tensor_scalar(target[:, t, :], xs[:, half, t, :], mv[:, t, 0:1],
                                                       st[:, 2, t:t + 1], ALU.subtract, ALU.mult)
                    last.then_inc(signal, 1)
                if piece == "scale":
                    await_root()
                    link(nc.vector.tensor_scalar(st[:, 0, :], ms[:], 1e-6, None, ALU.add))
                    refined_root()
                    v.wait_ge(pe_tr, PREP[step])
                    for t in range(NT):
                        last = nc.vector.tensor_scalar(hn[:, t, :], ys[:, half, t, :], st[:, 2, t:t + 1], None, ALU.mult)
                    last.then_inc(tok_ready, 1)
                if piece == "turn":
                    for k, bank in enumerate(turn_banks(u) if u else (bank_p, bank_t)):
                        v.wait_ge(xt_hi_ready, KD * PREP[step] + k + 1)
                        if kind == "x":
                            last = nc.vector.tensor_tensor(xt_lo[half][:, k, :], bank[:], xt_hi[half][:, k, :],
                                                           ALU.subtract)
                        else:
                            col = (SM_LN1 if kind == "y" else SM_LN2) + k
                            last = nc.vector.scalar_tensor_tensor(xt_lo[half][:, k, :], bank[:], sm[:, col:col + 1],
                                                                  xt_hi[half][:, k, :], ALU.mult, ALU.subtract)
                    last.then_inc(xt_lo_ready, 1)
                if piece == "logits":
                    v.wait_ge(pe_gate, half + 1)
                    logits = bank_p[:, 0:NT * E].rearrange("p (t e) -> p t e", e=E)
                    link(nc.vector.tensor_reduce(rmax[:, 0, :], logits, AX, ALU.max))
                    nc.vector.tensor_tensor(rt[:, 0], logits, per_expert(rmax[:, 0, :]), ALU.subtract).then_inc(logits_sub, 1)
                if piece == "equals":
                    v.wait_ge(logits_exp, half + 1)
                    link(nc.vector.tensor_reduce(rmax[:, 1, :], rt[:, 1], AX, ALU.add))
                    link(nc.vector.reciprocal(rmax[:, 2, :], rmax[:, 1, :]))
                    link(nc.vector.tensor_tensor(rt[:, 2], rt[:, 1], per_expert(rmax[:, 2, :]), ALU.mult))
                    link(nc.vector.tensor_tensor(pair1[:], others, mine, ALU.is_equal))
                if piece == "ties":
                    tie = sm[:, SM_TIE:SM_TIE + E * E].rearrange("p (e f) -> p e f", f=E).unsqueeze(1)
                    link(nc.vector.tensor_tensor(pair1[:], pair1[:], tie.to_broadcast([P, NT, E, E]), ALU.mult))
                if piece == "better":
                    link(nc.vector.tensor_tensor(pair2[:], others, mine, ALU.is_gt))
                if piece == "ranks":
                    link(nc.vector.tensor_tensor(pair1[:], pair1[:], pair2[:], ALU.add))
                if piece == "best":
                    link(nc.vector.tensor_reduce(rt[:, 3], pair1[:], AX, ALU.add))
                    link(nc.vector.tensor_scalar(rt[:, 4], rt[:, 3], float(TOP), None, ALU.is_lt))
                    link(nc.vector.tensor_tensor(rt[:, 5], rt[:, 4], rt[:, 2], ALU.mult))
                if piece == "weights":
                    link(nc.vector.tensor_reduce(rmax[:, 3, :], rt[:, 5], AX, ALU.add))
                    link(nc.vector.reciprocal(rmax[:, 1, :], rmax[:, 3, :]))
                    nc.vector.tensor_tensor(cw[:], rt[:, 5].unsqueeze(3).to_broadcast([P, NT, E, UNITS]),
                                            per_expert(rmax[:, 1, :]).unsqueeze(3).to_broadcast([P, NT, E, UNITS]),
                                            ALU.mult).then_inc(cw_ready, 1)
                if piece == "blend":
                    link(nc.vector.scalar_tensor_tensor(xs[:, half], ys[:, half], tg[:, 1:2], xs[:, half],
                                                        ALU.mult, ALU.add))

            def split_pv(u):
                stage = stages[u.kind]
                v.wait_ge(stage["pv_hi"], u.done())
                nc.vector.tensor_tensor(pv_lo[u.parity][:], bank_p[:], pv_hi[u.parity][:], ALU.subtract)\
                    .then_inc(stage["pv_lo"], 1)

            def softmax(u):
                stage = stages[u.kind]
                if u.kind == "a":
                    v.wait_ge(A["r_qk"], u.done())
                v.wait_ge(stage["scores"], u.done())
                found = tiles(bank_s[:, 0:NT * SEQ])
                if u.kind == "a":
                    nc.vector.tensor_tensor(sc[:], found, r_qk[:], ALU.mult).then_inc(A["scaled"], 1)
                else:
                    mask = sm[:, SM_MASK:SM_MASK + SEQ].unsqueeze(1).to_broadcast([P, NT, SEQ])
                    nc.vector.scalar_tensor_tensor(sc[:], found, SCALE, mask, ALU.mult, ALU.add).then_inc(B["scaled"], 1)
                v.wait_ge(stage["scaled"], u.done())
                nc.vector.tensor_reduce(sc_max[:], sc[:], AX, ALU.max).then_inc(stage["max"], 1)
                if u.prev() and u.prev().deferred:
                    split_pv(u.prev())
                v.wait_ge(stage["max"], u.done())
                nc.vector.tensor_tensor(sc_sub[:], sc[:], sc_max[:].unsqueeze(2).to_broadcast([P, NT, SEQ]),
                                        ALU.subtract).then_inc(stage["sub"], 1)
                v.wait_ge(stage["exp"], u.done())
                nc.vector.tensor_reduce(ex_sum[:], ex[:], AX, ALU.add).then_inc(stage["sum"], 1)
                v.wait_ge(stage["sum"], u.done())
                nc.vector.reciprocal(ex_inv[:], ex_sum[:]).then_inc(stage["inv"], 1)
                v.wait_ge(stage["inv"], u.done())
                for s, signal in ((0, stage["norm_lo"]), (1, stage["norm_hi"])):
                    rows = slice(s * SEQ, (s + 1) * SEQ)
                    nc.vector.tensor_tensor(attn[rows, :, s * SEQ:(s + 1) * SEQ], ex[rows],
                                            ex_inv[rows].unsqueeze(2).to_broadcast([SEQ, NT, SEQ]), ALU.mult)\
                        .then_inc(signal, 1)

            def take_q(u):
                if u.kind == "a":
                    v.wait_ge(A["sq_q"], u.done())
                    nc.vector.tensor_copy(qt[:], bank_q[:]).then_inc(A["qt"], 1)
                if u.kind == "b":
                    v.wait_ge(B["q_done"], u.done())
                    nc.vector.tensor_copy(qt[:], bank_q[:]).then_inc(B["qt"], 1)

            def split_first(u, user):
                if user:
                    v.wait_ge(M["g_done"] if user.kind == "m" else stages[user.kind]["q_done"], user.done())
                if u.kind == "a":
                    v.wait_ge(ld_a1[u.parity], u.loads())
                    nc.vector.tensor_copy(wq_hi[u.parity][:], raw_a1[u.parity][:, AQ:AQ + D]).then_inc(A["wq_hi"], 1)
                elif u.kind == "b":
                    v.wait_ge(ld_b1[u.parity], u.loads())
                    nc.vector.tensor_copy(wq_hi[u.parity][:], raw_b1[u.parity][:, 0:D]).then_inc(B["wq_hi"], 1)
                else:
                    v.wait_ge(ld_m1[u.parity], u.loads())
                    nc.vector.tensor_copy(wq_hi[u.parity][:], raw_m1[u.parity][:, MG:MG + D]).then_inc(M["wg_hi"], 1)

            def split_second(u, user):
                if user:
                    v.wait_ge(M["u_done"] if user.kind == "m" else stages[user.kind]["k_done"], user.done())
                if u.kind == "a":
                    nc.vector.tensor_copy(wk_hi[u.parity][:, 0:P], raw_a1[u.parity][:, AK:AK + P]).then_inc(A["wk_hi"], 1)
                elif u.kind == "b":
                    nc.vector.tensor_copy(wk_hi[u.parity][:], raw_b1[u.parity][:, D:2 * D]).then_inc(B["wk_hi"], 1)

            def split_values(first):
                number = first.pair_number()
                if not first.very_first:
                    v.wait_ge(B["v_done"], (number - 1) * 2)
                v.wait_ge(ld_v, number * 16)
                nc.vector.tensor_copy(wv_hi[:], raw_v[:]).then_inc(B["wv_hi"], 1)

            def split_out(u):
                if not u.in_first_pair:
                    v.wait_ge(B["wo_done"], u.done(2))
                v.wait_ge(ld_b2[u.parity], u.loads())
                nc.vector.tensor_copy(wo_hi[u.parity][:], raw_b2[u.parity][:]).then_inc(B["wo_hi"], 1)

            def weigh_gate(u):
                if u.needs_tokens:
                    v.wait_ge(unit_w_ready, u.half + 1)
                if u.static and u.i >= CH - SHARED:
                    weights = ones[:].to_broadcast([P, HT])
                else:
                    weights = unit_w[u.half][:, u.offset % GROUPS, :]
                v.wait_ge(M["silu"], u.done())
                nc.vector.tensor_tensor(gu[:], gs[:], weights, ALU.mult).then_inc(M["weighted"], 1)

            def multiply_up(u):
                v.wait_ge(M["weighted"], u.done())
                v.wait_ge(M["u_done"], u.done())
                if not u.very_first:
                    v.wait_ge(M["hh_hi"], u.done(1))
                nc.vector.tensor_tensor(hh[:], up_bank(u)[:], gu[:], ALU.mult).then_inc(M["hh"], 1)

            def split_hidden(u):
                v.wait_ge(M["hh_hi"], u.done())
                nc.vector.tensor_tensor(pv_lo[u.parity][:], hh[:], pv_hi[u.parity][:], ALU.subtract).then_inc(M["hh_lo"], 1)

            def read_acc(last):
                kind, half = last.kind, last.half
                for b in range(2):
                    two = slice(2 * b, 2 * b + 2)
                    part = acc[b][:].rearrange("p (t d) -> p t d", d=D)
                    if kind == "m" and b == 0:
                        v.wait_ge(down_part, half + 1)
                    else:
                        v.wait_ge(stages[kind]["down" if kind == "m" else "wo_done"], last.done())
                    if kind == "b":
                        add = nc.vector.tensor_tensor(ys[:, half, two], part, ys[:, half, two], ALU.add)
                    else:
                        gate = tg[:, 0:1] if kind == "a" else tg[:, 1:2]
                        add = nc.vector.scalar_tensor_tensor(xs[:, half, two], part, gate, xs[:, half, two],
                                                             ALU.mult, ALU.add)
                    add.then_inc(out_ready if kind == "m" else acc_free, 1)
                if kind != "m":
                    v.wait_ge(acc_free, STAGES.index((kind, half)) * 2 + 2)

            def head(u):
                prev, nxt = u.prev(), u.next()
                after = nxt.next()
                softmax(u)
                turning = piece_at(u)[0] == "turn"
                if turning:
                    prepare_piece(*piece_at(u), u)
                take_q(nxt)
                split_first(after, u)
                if after.kind != "m":
                    split_second(after, u)
                if nxt.kind == "m":
                    weigh_gate(nxt)
                    multiply_up(nxt)
                if u.first and prev:
                    read_acc(prev)
                if not turning:
                    prepare_piece(*piece_at(u), u)
                if u.kind == "b":
                    split_out(u)
                if u.kind == "a" and u.half == 0:
                    v.wait_ge(A["vo_hi"], u.done())
                    this = bass.ds(u.i, 1)
                    nc.vector.tensor_tensor(vo_lo[:, this, :].squeeze(1), bank_v[:, 0:D], vo_hi[:, this, :].squeeze(1),
                                            ALU.subtract).then_inc(A["vo_lo"], 1)
                if after.kind == "b" and not after.odd:
                    split_values(after)
                if not u.deferred:
                    split_pv(u)

            def chunk(u):
                nxt = u.next()
                after = nxt.next() if nxt else None
                if u.very_first:
                    split_hidden(u)
                if after:
                    split_first(after, u)
                if u.very_first:
                    read_acc(u.prev())
                with_scalar = piece_at(u)[0] in ("turn", "logits", "spread")
                if not with_scalar:
                    prepare_piece(*piece_at(u), u)
                if nxt:
                    weigh_gate(nxt)
                    multiply_up(nxt)
                if nxt:
                    split_hidden(nxt)
                if with_scalar:
                    prepare_piece(*piece_at(u), u)
                if u.last:
                    read_acc(u)

            prepare_piece("stats", ("x", 0))
            v.wait_ge(ld_small, 16)
            v.wait_ge(setup_pool, SETUP)
            nc.vector.scalar_tensor_tensor(gqk[:], sm[:, SM_GQ:SM_GQ + 1], SCALE, sm[:, SM_GK:SM_GK + 1],
                                           ALU.mult, ALU.mult).then_inc(setup_dve, 1)
            start = first_unit("a", 0)
            split_first(start, None)
            split_second(start, None)
            v.wait_ge(setup_act, 1)
            prepare_piece("norm", ("x", 0))
            prepare_piece("turn", ("x", 0))
            take_q(start)
            split_first(start.next(), None)
            split_second(start.next(), None)
            for kind, half in STAGES:
                run_units(v, kind, half, chunk if kind == "m" else head)

        @block.gpsimd
        def _(pool):
            def rest(lo, raw, hi, signal):
                nc.gpsimd.tensor_tensor(lo, raw, hi, ALU.subtract).then_inc(signal, 1)

            def split_first(u):
                if u.kind == "a":
                    pool.wait_ge(A["wq_hi"], u.done())
                    rest(wq_lo[u.parity][:], raw_a1[u.parity][:, AQ:AQ + D], wq_hi[u.parity][:], A["wq_lo"])
                elif u.kind == "b":
                    pool.wait_ge(B["wq_hi"], u.done())
                    rest(wq_lo[u.parity][:], raw_b1[u.parity][:, 0:D], wq_hi[u.parity][:], B["wq_lo"])
                else:
                    pool.wait_ge(M["wg_hi"], u.done())
                    rest(wq_lo[u.parity][:], raw_m1[u.parity][:, MG:MG + D], wq_hi[u.parity][:], M["wg_lo"])

            def split_second(u):
                if u.kind == "a":
                    pool.wait_ge(A["wk_hi"], u.done())
                    rest(wk_lo[u.parity][:, 0:P], raw_a1[u.parity][:, AK:AK + P], wk_hi[u.parity][:, 0:P], A["wk_lo"])
                elif u.kind == "b":
                    pool.wait_ge(B["wk_hi"], u.done())
                    rest(wk_lo[u.parity][:], raw_b1[u.parity][:, D:2 * D], wk_hi[u.parity][:], B["wk_lo"])
                else:
                    pool.wait_ge(M["wu_hi"], u.done())
                    rest(wk_lo[u.parity][:], raw_m1[u.parity][:, MU:MU + D], wk_hi[u.parity][:], M["wu_lo"])

            def split_values(first):
                pool.wait_ge(B["wv_hi"], first.pair_number())
                rest(wv_lo[:], raw_v[:], wv_hi[:], B["wv_lo"])

            def split_out(u):
                if u.kind == "b":
                    pool.wait_ge(B["wo_hi"], u.done())
                    rest(wo_lo[u.parity][:], raw_b2[u.parity][:], wo_hi[u.parity][:], B["wo_lo"])
                else:
                    pool.wait_ge(M["wd_hi"], u.done())
                    rest(wo_lo[u.parity][:], raw_m2[u.parity][:], wo_hi[u.parity][:], M["wd_lo"])

            def split_squares(u):
                if u.kind == "a":
                    pool.wait_ge(A["sq_k_hi"], u.done())
                    rest(sq_k_lo[:], sq_k[:], sq_k_hi[:], A["sq_k_lo"])

            def add_logs(u):
                pool.wait_ge(A["ln_k"], u.done())
                pool.wait_ge(A["ln_q"], u.done())
                nc.gpsimd.tensor_tensor(ln_qk[:], ln_k[:], ln_q[:].unsqueeze(2).to_broadcast([P, NT, SEQ]), ALU.add)\
                    .then_inc(A["ln_qk"], 1)

            def head(u):
                nxt = u.next()
                after = nxt.next()
                split_squares(nxt)
                split_first(after)
                split_second(after)
                if nxt.kind == "a":
                    add_logs(nxt)
                if u.kind == "b":
                    split_out(u)
                if after.kind == "b" and not after.odd:
                    split_values(after)
            
            def chunk(u):
                nxt = u.next()
                after = nxt.next() if nxt else None
                if u.very_first:
                    split_out(u)
                if after:
                    split_first(after)
                    split_second(after)
                if nxt:
                    split_out(nxt)

            nc.gpsimd.memset(zeros[:].bitcast(F32), 0.0).then_inc(setup_pool, 1)
            nc.gpsimd.memset(ones[:], 1.0).then_inc(setup_pool, 1)
            nc.gpsimd.memset(attn[:], 0.0).then_inc(setup_pool, 1)
            nc.gpsimd.memset(eps5[:], 1e-5).then_inc(setup_pool, 1)
            nc.gpsimd.memset(eps6[:], 1e-6).then_inc(setup_pool, 1)
            nc.gpsimd.memset(ones_of[:].bitcast(F32), 0.0).then_inc(setup_pool, 1)
            pool.wait_ge(setup_pool, SETUP - SPB)
            for s in range(SPB):
                nc.gpsimd.memset(ones_of[:, s, s * SEQ:(s + 1) * SEQ].bitcast(F32), 1.0).then_inc(setup_pool, 1)
            def split_context(half):
                pool.wait_ge(ctxt_hi_ready, half + 1)
                toks = slice(half * HT, (half + 1) * HT)
                rest(ctxt_lo[:, toks], ctxt[:, toks], ctxt_hi[:, toks], ctxt_lo_ready)

            start = first_unit("a", 0)
            split_first(start)
            split_second(start)
            split_context(0)
            split_squares(start)
            split_first(start.next())
            split_second(start.next())
            add_logs(start)
            split_context(1)
            for kind, half in STAGES:
                run_units(pool, kind, half, chunk if kind == "m" else head)


_INS = ["x", "ctx_t", "ctx", "head_a", "head_b", "pair_v", "chunk_m", "small"]


def lay_out(i, np):
    a = {k: np.asarray(v) for k, v in i.items()}
    f = np.float32
    x = a["x"].reshape(-1, a["x"].shape[-1])
    D = x.shape[1]
    ctx = a["ctx_1024"].reshape(x.shape[0], -1)
    C = ctx.shape[1]
    K = D // P

    def in_heads(w, chunks):
        h = w.shape[1] // P
        return w.reshape(chunks, P, h, P).transpose(2, 1, 0, 3).reshape(h, P, chunks * P)

    def out_heads(w):
        return w.reshape(-1, P, w.shape[1])

    wv_t = a["L0_xattn_Wv"].reshape(C, -1, P).transpose(1, 2, 0)
    head_a = np.concatenate([in_heads(a["L0_xattn_Wq"], K), in_heads(a["L0_xattn_Wk"], 1), wv_t,
                             out_heads(a["L0_xattn_Wo"])], axis=2)
    head_b = np.concatenate([in_heads(a["L0_ffn_wq"], K), in_heads(a["L0_ffn_wk"], K),
                             out_heads(a["L0_ffn_wo"])], axis=2)
    wv = a["L0_ffn_wv"]
    pair_v = wv.reshape(K, P, -1, 2 * P).transpose(2, 1, 0, 3).reshape(-1, P, K * 2 * P)
    E, I, _ = a["L0_ffn_eg_w"].shape
    units = 2 * P // E

    def in_chunks(experts, shared):
        e = experts.reshape(2, E // 2, I // units, units, D).transpose(2, 0, 1, 3, 4).reshape(E * I, D)
        pad = np.zeros((-shared.shape[0] % P, D), f)
        return np.concatenate([e, shared, pad])

    gate = in_chunks(a["L0_ffn_eg_w"], a["L0_ffn_sg_w"])
    up = in_chunks(a["L0_ffn_eu_w"], a["L0_ffn_su_w"])
    down = in_chunks(a["L0_ffn_ed_w"].transpose(0, 2, 1), a["L0_ffn_sd_w"].T)
    chunk_m = np.concatenate([in_heads(gate.T, K), in_heads(up.T, K), down.reshape(-1, P, D)], axis=2)
    query, key = np.arange(P)[:, None] % SEQ, np.arange(SEQ)[None]
    mask = np.where(key <= query, f(0), f(-1e30)).astype(f)
    tie = np.tril(np.ones((E, E), f), -1).reshape(1, -1)
    small = np.concatenate([
        a["L0_xattn_gq"].reshape(P, 1), a["L0_xattn_gk"].reshape(P, 1),
        a["L0_ffn_ln1_w"].reshape(K, P).T, a["L0_ffn_ln2_w"].reshape(K, P).T,
        np.broadcast_to(a["g_xattn"].reshape(1, 1), (P, 1)), np.broadcast_to(a["g_ffn"].reshape(1, 1), (P, 1)),
        a["L0_ffn_gate_w"].T.reshape(K, P, E).transpose(1, 0, 2).reshape(P, K * E),
        np.eye(P, dtype=f), mask, np.broadcast_to(tie, (P, E * E))], axis=1)
    return {"x": x, "ctx_t": ctx.T, "ctx": ctx, "head_a": head_a, "head_b": head_b, "pair_v": pair_v,
            "chunk_m": chunk_m, "small": small}


def kernel(**inputs):
    import concourse.bacc as bacc
    import numpy as np
    from concourse.bass_utils import run_bass_kernel_spmd

    laid = {k: np.ascontiguousarray(v) for k, v in lay_out(inputs, np).items()}
    nc = bacc.Bacc("TRN2", target_bir_lowering=False, num_devices=1)
    aps = [nc.dram_tensor(f"in_{n}", laid[n].shape, mybir.dt.from_np(laid[n].dtype), kind="ExternalInput").ap() for n in _INS]
    out = nc.dram_tensor("out", laid["x"].shape, F32, kind="ExternalOutput").ap()
    flamingo_layer(nc, *aps, out, inputs["L0_ffn_sg_w"].shape[0])
    r = run_bass_kernel_spmd(nc, [{f"in_{n}": laid[n] for n in _INS}], core_ids=[0])
    return r.results[0]["out"].reshape(inputs["x"].shape)
```
